# Optimizing a Trainium2 kernel written in Bass

```python
import numpy as np
import jax
import jax.numpy as jnp

def _softmax(x, axis=-1):
    return jax.nn.softmax(x, axis=axis)

def _gelu(x):
    return jax.nn.gelu(x, approximate=True)

def _silu(x):
    return jax.nn.silu(x)

def _sigmoid(x):
    return jax.nn.sigmoid(x)

def _layernorm(x, axis=-1, eps=1e-05):
    m = jnp.mean(x, axis=axis, keepdims=True)
    v = jnp.var(x, axis=axis, keepdims=True)
    return (x - m) / jnp.sqrt(v + eps)

def _scatter_add(tgt, idx, src, axis=0):
    return tgt.at[idx].add(src)

def _segment_sum(src, seg, n):
    return jax.ops.segment_sum(src, seg, n)
kernel_name = 'mk_flamingo_gated_d1_seqx_r4_7100e9'

def setup_inputs(seed: int=0):
    np.random.seed(seed)
    _w = jnp.asarray

    def _rec_inputs():
        import jax
        import jax.numpy as jnp
        _rk = jax.random.key(seed)
        x = -0.0002928 + 1 * jax.random.normal(jax.random.fold_in(_rk, 1), (32, 112, 256), jnp.float32)
        _lenS = 112 - jax.random.randint(jax.random.fold_in(_rk, 7), (32,), 0, max(1, 112 // 4) + 1, jnp.int32)
        _lenS2 = 375 - jax.random.randint(jax.random.fold_in(_rk, 8), (32,), 0, max(1, 375 // 4) + 1, jnp.int32)
        _ctx_1024P = jax.random.normal(jax.random.fold_in(_rk, 11), (32, 16, 256), jnp.float32)
        _ctx_1024c = jax.random.dirichlet(jax.random.fold_in(_rk, 511), 0.3 * jnp.ones((16,), jnp.float32), (32, 375))
        _ctx_1024t = jnp.einsum('bsk,bkd->bsd', _ctx_1024c, _ctx_1024P)
        _ctx_1024t = _ctx_1024t * jax.lax.rsqrt(jnp.mean(jnp.square(_ctx_1024t)) + 1e-12) * 0.953939
        ctx_1024 = -1.39393e-06 + 0.999914 * (_ctx_1024t + 0.3 * jax.random.normal(jax.random.fold_in(_rk, 611), (32, 375, 256), jnp.float32))
        _g = jax.random.normal(jax.random.fold_in(_rk, 9001), (2, 1), jnp.float32)
        _g = jnp.sign(_g) * jnp.maximum(jnp.abs(_g), 1.0) + (_g == 0) * 1.0
        g_xattn = _g[0]
        g_ffn = _g[1]
        return (x, ctx_1024, g_xattn, g_ffn)
    x, ctx_1024, g_xattn, g_ffn = _rec_inputs()

    def _L0_xattn_setup():
        import jax, jax.numpy as jnp
        import numpy as np
        D_MODEL = 256
        NUM_HEADS = 16
        DEPTH = D_MODEL // NUM_HEADS

        def _split_heads(x):
            B, S, _ = x.shape
            return x.reshape(B, S, NUM_HEADS, DEPTH).transpose(0, 2, 1, 3)
        key = jax.random.key(seed)
        ks = jax.random.split(key, 11)
        B, S = (2, 512)
        scale = 1.0 / np.sqrt(D_MODEL)
        inp = {'q': jax.random.normal(ks[0], (B, S, D_MODEL), jnp.float32), 'k': jax.random.normal(ks[1], (B, S, D_MODEL), jnp.float32), 'v': jax.random.normal(ks[2], (B, S, D_MODEL), jnp.float32), 'wq': jax.random.normal(ks[3], (D_MODEL, D_MODEL), jnp.float32) * scale, 'bq': jnp.zeros((D_MODEL,), jnp.float32), 'wk': jax.random.normal(ks[4], (D_MODEL, D_MODEL), jnp.float32) * scale, 'bk': jnp.zeros((D_MODEL,), jnp.float32), 'wv': jax.random.normal(ks[5], (D_MODEL, D_MODEL), jnp.float32) * scale, 'bv': jnp.zeros((D_MODEL,), jnp.float32), 'wo': jax.random.normal(ks[6], (D_MODEL, D_MODEL), jnp.float32) * scale, 'bo': jnp.zeros((D_MODEL,), jnp.float32)}
        return inp
    _L0_xattn_all = _L0_xattn_setup()
    _L0_xattn_in = {k: v for k, v in _L0_xattn_all.items() if k in ('wq', 'bq', 'wk', 'bk', 'wv', 'bv', 'wo', 'bo')}
    del _L0_xattn_all

    def _L0_ffn_setup():
        import jax, jax.numpy as jnp
        import numpy as np
        NUM_EXPERTS = 8
        TOP_K = 2
        key = jax.random.key(seed)
        ks = jax.random.split(key, 4)
        B, S, H, F = (4, 1024, 256, 1024)
        x = jax.random.normal(ks[0], (B, S, H), dtype=jnp.float32)
        router_w = jax.random.normal(ks[1], (H, NUM_EXPERTS), dtype=jnp.float32) * 0.02
        w1 = jax.random.normal(ks[2], (H, F), dtype=jnp.float32) * 0.02
        b1 = jnp.zeros((F,), dtype=jnp.float32)
        w2 = jax.random.normal(ks[3], (F, H), dtype=jnp.float32) * 0.02
        b2 = jnp.zeros((H,), dtype=jnp.float32)
        return {'x': x, 'router_w': router_w, 'w1': w1, 'b1': b1, 'w2': w2, 'b2': b2}
    _L0_ffn_all = _L0_ffn_setup()
    _L0_ffn_in = {k: v for k, v in _L0_ffn_all.items() if k in ('router_w', 'w1', 'b1', 'w2', 'b2')}
    del _L0_ffn_all
    return {'x': x, 'ctx_1024': ctx_1024, 'g_xattn': g_xattn, 'g_ffn': g_ffn, 'L0_xattn_wq': _L0_xattn_in['wq'], 'L0_xattn_bq': _L0_xattn_in['bq'], 'L0_xattn_wk': _L0_xattn_in['wk'], 'L0_xattn_bk': _L0_xattn_in['bk'], 'L0_xattn_wv': _L0_xattn_in['wv'], 'L0_xattn_bv': _L0_xattn_in['bv'], 'L0_xattn_wo': _L0_xattn_in['wo'], 'L0_xattn_bo': _L0_xattn_in['bo'], 'L0_ffn_router_w': _L0_ffn_in['router_w'], 'L0_ffn_w1': _L0_ffn_in['w1'], 'L0_ffn_b1': _L0_ffn_in['b1'], 'L0_ffn_w2': _L0_ffn_in['w2'], 'L0_ffn_b2': _L0_ffn_in['b2']}

def reference(x, ctx_1024, g_xattn, g_ffn, L0_xattn_wq, L0_xattn_bq, L0_xattn_wk, L0_xattn_bk, L0_xattn_wv, L0_xattn_bv, L0_xattn_wo, L0_xattn_bo, L0_ffn_router_w, L0_ffn_w1, L0_ffn_b1, L0_ffn_w2, L0_ffn_b2):
    import jax
    import jax.numpy as jnp

    def _L0_xattn_ref(q, k, v, wq, bq, wk, bk, wv, bv, wo, bo):
        import jax, jax.numpy as jnp
        import numpy as np
        D_MODEL = 256
        NUM_HEADS = 16
        DEPTH = D_MODEL // NUM_HEADS

        def _split_heads(x):
            B, S, _ = x.shape
            return x.reshape(B, S, NUM_HEADS, DEPTH).transpose(0, 2, 1, 3)
        B, S, _ = q.shape
        qh = _split_heads(q @ wq + bq)
        kh = _split_heads(k @ wk + bk)
        vh = _split_heads(v @ wv + bv)
        logits = jnp.einsum('bhqd,bhkd->bhqk', qh, kh) / jnp.sqrt(jnp.asarray(DEPTH, qh.dtype))
        attn = jax.nn.softmax(logits, axis=-1)
        out = jnp.einsum('bhqk,bhkd->bhqd', attn, vh)
        out = out.transpose(0, 2, 1, 3).reshape(B, S, D_MODEL)
        return out @ wo + bo

    def _L0_ffn_ref(x, router_w, w1, b1, w2, b2):
        import jax, jax.numpy as jnp
        import numpy as np
        NUM_EXPERTS = 8
        TOP_K = 2
        B, S, H = x.shape
        xt = x.reshape(-1, H)
        router_logits = jnp.matmul(xt, router_w)
        router_probs = jax.nn.softmax(router_logits, axis=-1)
        top_k_probs, top_k_indices = jax.lax.top_k(router_probs, TOP_K)
        top_k_probs = top_k_probs / jnp.sum(top_k_probs, axis=-1, keepdims=True)
        one_hot = jax.nn.one_hot(top_k_indices, NUM_EXPERTS, dtype=xt.dtype)
        combine = jnp.einsum('tk,tke->te', top_k_probs, one_hot)
        expert_out = jnp.matmul(jax.nn.gelu(jnp.matmul(xt, w1) + b1), w2) + b2
        out = expert_out * jnp.sum(combine, axis=-1, keepdims=True)
        return out.reshape(B, S, H)
    x = x + jnp.tanh(g_xattn[0]) * _L0_xattn_ref(_layernorm(x, axis=-1), ctx_1024, ctx_1024, L0_xattn_wq, L0_xattn_bq, L0_xattn_wk, L0_xattn_bk, L0_xattn_wv, L0_xattn_bv, L0_xattn_wo, L0_xattn_bo)
    x = x + jnp.tanh(g_ffn[0]) * _L0_ffn_ref(_layernorm(x, axis=-1), L0_ffn_router_w, L0_ffn_w1, L0_ffn_b1, L0_ffn_w2, L0_ffn_b2)
    return x

_drawn_inputs = setup_inputs


def setup_inputs(seed=0):
    import zlib

    import numpy as np

    out = dict(_drawn_inputs(seed))
    spreads = {'L0_xattn_bq': (0.0, 0.49),
     'L0_xattn_bk': (0.0, 0.8),
     'L0_xattn_bv': (0.0, 0.1),
     'L0_xattn_bo': (0.0, 0.1),
     'L0_ffn_b1': (0.0, 0.1),
     'L0_ffn_b2': (0.0, 0.1)}
    factors = {'L0_ffn_router_w': 8.0}
    for name, (base, spread) in spreads.items():
        noise = np.random.default_rng([zlib.crc32(name.encode()), seed]).standard_normal(out[name].shape)
        drawn = base * np.exp(spread * noise) if base else spread * noise
        out[name] = jnp.asarray(drawn.astype(out[name].dtype))
    for name, factor in factors.items():
        out[name] = (out[name] * factor).astype(out[name].dtype)
    return out
```

```python
from contextlib import ExitStack

import concourse.bass as bass
from concourse import mybir

F32 = mybir.dt.float32
F32R = mybir.dt.float32r
ALU = mybir.AluOpType
ACT = mybir.ActivationFunctionType
AX = mybir.AxisListType

NB, SQ, D = 32, 112, 256
SK = 375
SKP = SK + 1
NH, DH = 16, 16
NPAIR = NH // 2
FF, NE = 1024, 8
GB = 4
NG = NB // GB
TOK = GB * SQ
DC = D // 128
FC = FF // 128
KC, KN = 3, SK // 3
SCALE = float(DH) ** -0.5
EPS = 1e-5
RING = 4
VW = DH + 1


class At:

    def __init__(self, it, k):
        self.it, self.k = it, k
        self.j = k % GB
        self.ring = k % RING
        self.par = k % 2
        self.gpar = (k // GB) % 2
        self.exists = not isinstance(it, int) or 0 <= k < NB

    def shift(self, d):
        return At(self.it, self.k + d)

    def count(self, per, off=0):
        return self.it * (8 * per) + self.k * per + off

    def group(self, per=1, off=0):
        return self.it * (2 * per) + (self.k // GB) * per + off

    def half(self, per, off=0):
        return self.it * (4 * per) + (self.k // 2) * per + off


def past(value):
    return not isinstance(value, int) or value > 0


def held(engine, passed, *waits):
    for s, v in waits:
        if past(v):
            engine.wait_ge(s, v)
            engine.sem_inc(passed, 1)


def build(nc, x, ctxT, g_xattn, g_ffn, wq, bq, wk, bk, wv, bv, wo, bo, wr, w1, b1, w2, b2, out):
    with ExitStack() as ctx:
        def sb(name, shape, dt=F32):
            return ctx.enter_context(nc.sbuf_tensor(name, shape, dt))

        def ps(name):
            return ctx.enter_context(nc.psum_tensor(name, [128, 512], F32))

        def sem(name):
            return ctx.enter_context(nc.semaphore(name))

        WQ = sb("WQ", [128, DC, D])
        WK = sb("WK", [128, DC, D])
        WV = sb("WV", [128, DC, D])
        WO = sb("WO", [128, 4, D])
        WR = sb("WR", [128, DC, NE])
        W1 = sb("W1", [128, DC, FF])
        W2 = sb("W2", [128, FC, D])
        BQ = sb("BQ", [128, DC])
        BK = sb("BK", [128, DC])
        B1 = sb("B1", [128, FC])
        BV = sb("BV", [KN, D])
        BO = sb("BO", [SQ, D])
        B2 = sb("B2", [SQ, D])
        GATE = sb("GATE", [128, 2])
        TG = sb("TG", [128, 2])
        IDENT = sb("IDENT", [128, 128])
        MHALF = sb("MHALF", [SQ, GB])

        X = sb("X", [SQ, 2, GB, D])
        CT = sb("CT", [128, 2, DC, SK])
        BST1 = sb("BST1", [SQ, GB, 6])
        MV1 = sb("MV1", [SQ, GB, 2])
        VE1 = sb("VE1", [SQ, GB])
        RSTD1 = sb("RSTD1", [SQ, GB])
        XN = sb("XN", [SQ, GB, D])
        XNT = sb("XNT", [128, DC, TOK])

        QHI = sb("QHI", [128, DC, TOK], F32R)
        QLO = sb("QLO", [128, DC, TOK], F32R)
        QS = sb("QS", [128, NH, RING * SQ], F32R)
        KHI = sb("KHI", [128, DC, SK], F32R)
        KLO = sb("KLO", [128, DC, SK], F32R)
        KS = sb("KS", [128, RING, NPAIR, SKP], F32R)
        VA = sb("VA", [KN, RING, KC, NH, VW])
        NEGM = sb("NEGM", [SQ, 2, NH])
        MHI = sb("MHI", [NH, SQ], F32R)
        MLO = sb("MLO", [NH, SQ], F32R)
        PT = sb("PT", [KN, KC, NH * SQ])
        RSUM = sb("RSUM", [128, TOK])
        RINV = sb("RINV", [128, TOK])
        AT = sb("AT", [128, 4, SQ])

        X1 = sb("X1", [SQ, 2, GB, D])
        BST2 = sb("BST2", [SQ, GB, 6])
        MV2 = sb("MV2", [SQ, 2, GB, 2])
        VE2 = sb("VE2", [SQ, GB])
        RSTD2 = sb("RSTD2", [SQ, GB])
        X2N = sb("X2N", [SQ, GB, D])
        X2NT = sb("X2NT", [128, DC, TOK])
        HT = sb("HT", [128, FC, TOK])
        LG = sb("LG", [SQ, GB, NE])
        SORTED = sb("SORTED", [SQ, GB, NE])
        DIFF = sb("DIFF", [SQ, GB, NE])
        ER = sb("ER", [SQ, GB, NE])
        ZR = sb("ZR", [SQ, 4, GB])
        PR = sb("PR", [SQ, GB, 2])
        WN = sb("WN", [SQ, GB, 2])
        WS = sb("WS", [SQ, GB])
        WT = sb("WT", [SQ, GB])
        B2W = sb("B2W", [SQ, D])

        KD = nc.dram_tensor("k_parts", (2, 2, NPAIR, 32, SK), F32, kind="Internal").ap()
        QD = nc.dram_tensor("q_parts", (2, 2, DC, 4, DH, TOK), F32, kind="Internal").ap()

        S_BANK = [ps("S0"), ps("S1")]
        T_BANK = [ps("T0"), ps("T1")]
        P_BANK = [ps("P0"), ps("P1")]
        OT = ps("OT")
        TR = ps("TR")

        sp_passed = sem("sp_passed")
        dve_passed = sem("dve_passed")
        pool_passed = sem("pool_passed")
        w_loaded = sem("w_loaded")
        x_loaded = [sem("x_loaded0"), sem("x_loaded1")]
        ct_loaded = [sem("ct_loaded0"), sem("ct_loaded1")]
        pool_zeroed = sem("pool_zeroed")
        dve_zeroed = sem("dve_zeroed")
        tanh_done = sem("tanh_done")
        bo_done = sem("bo_done")
        ident_done = sem("ident_done")
        stats1_done = sem("stats1_done")
        mv1_done = sem("mv1_done")
        ve1_done = sem("ve1_done")
        rstd1_done = sem("rstd1_done")
        xn_done = sem("xn_done")
        xb_done = sem("xb_done")
        xt_ready = sem("xt_ready")
        xt_done = sem("xt_done")
        q_ready = sem("q_ready")
        qhi_done = sem("qhi_done")
        qlo_done = sem("qlo_done")
        qs_loaded = sem("qs_loaded")
        k_ready = sem("k_ready")
        khi_done = sem("khi_done")
        klo_done = sem("klo_done")
        ks_loaded = sem("ks_loaded")
        khi_stored = sem("khi_stored")
        klo_stored = sem("klo_stored")
        qhi_stored = sem("qhi_stored")
        qlo_stored = sem("qlo_stored")
        v_ready = sem("v_ready")
        v_done = sem("v_done")
        s_ready = sem("s_ready")
        max_done = sem("max_done")
        mt_ready = sem("mt_ready")
        mhi_done = sem("mhi_done")
        mlo_done = sem("mlo_done")
        m_loaded = sem("m_loaded")
        st_ready = sem("st_ready")
        exp_done = sem("exp_done")
        pv_done = sem("pv_done")
        rsum_done = sem("rsum_done")
        rinv_done = sem("rinv_done")
        at_done = sem("at_done")
        wo_ready = sem("wo_ready")
        x1_done = sem("x1_done")
        stats2_done = sem("stats2_done")
        mv2_done = sem("mv2_done")
        ve2_done = sem("ve2_done")
        rstd2_done = sem("rstd2_done")
        x2n_done = sem("x2n_done")
        x2t_ready = sem("x2t_ready")
        x2t_done = sem("x2t_done")
        up_ready = sem("up_ready")
        gelu_done = sem("gelu_done")
        lg_ready = sem("lg_ready")
        lg_done = sem("lg_done")
        sort_done = sem("sort_done")
        diff_done = sem("diff_done")
        er_done = sem("er_done")
        zr_done = sem("zr_done")
        pr_done = sem("pr_done")
        wn_done = sem("wn_done")
        ws_done = sem("ws_done")
        wt_done = sem("wt_done")
        b2w_done = sem("b2w_done")
        x1b_done = sem("x1b_done")
        dn_ready = sem("dn_ready")
        y_done = sem("y_done")
        out_stored = sem("out_stored")

        QS_LOADS = 3 * 2
        N_WEIGHTS = 3 + 3 + 3 + 2 + 4 + 3

        block = ctx.enter_context(nc.Block())

        def run(engine, step, enter=None):
            for k in range(-2, GB):
                step(At(0, k))
            with engine.Fori(0, (NG - 2) // 2) as it:
                for k in range(GB, 3 * GB):
                    if enter and k % GB == 0:
                        enter(At(it, k))
                    step(At(it, k))
            for k in range(NB - GB, NB + GB):
                if enter and k == NB - GB:
                    enter(At(0, k))
                step(At(0, k))

        @block.sync
        def _(sp):
            for dst, src in ((WK, wk), (WV, wv), (WQ, wq)):
                sp.dma_start(dst[:, :, :], src.rearrange("(c p) n -> p c n", p=128)).then_inc(w_loaded, 16)
            sp.dma_start(CT[:, 0, :, :], ctxT[0].rearrange("p (c n) -> p c n", c=DC)).then_inc(ct_loaded[0], 16)
            sp.dma_start(X[:, 0, :, :], x[0:GB].rearrange("j q d -> q j d")).then_inc(x_loaded[0], 16)
            for dst, src in ((BQ, bq), (BK, bk), (B1, b1)):
                sp.dma_start(dst[:, :], src).then_inc(w_loaded, 16)
            for dst, src, n in ((BV, bv, KN), (BO, bo, SQ), (B2, b2, SQ)):
                sp.dma_start(dst[:, :], src.partition_broadcast(n)).then_inc(w_loaded, 16)
            for i, src in enumerate((g_xattn, g_ffn)):
                sp.dma_start(GATE[:, i:i + 1], src.partition_broadcast(128)).then_inc(w_loaded, 16)
            sp.wait_ge(pool_zeroed, 1)
            for j in range(4):
                sp.dma_start(WO[32 * j:32 * j + DH, :, :],
                             wo.rearrange("(s j d) n -> j d s n", s=4, j=4)[j]).then_inc(w_loaded, 16)
            sp.dma_start(WR[:, :, :], wr.rearrange("(c p) n -> p c n", p=128)).then_inc(w_loaded, 16)
            sp.dma_start(W1[:, :, :], w1.rearrange("(c p) n -> p c n", p=128)).then_inc(w_loaded, 16)
            sp.dma_start(W2[:, :, :], w2.rearrange("(c p) n -> p c n", p=128)).then_inc(w_loaded, 16)
            sp.wait_ge(pool_zeroed, 4)
            sp.wait_ge(dve_zeroed, 3)

            def at(first, n):
                return slice(first, first + n) if isinstance(first, int) else bass.ds(sp.snap(first), n)

            def stack_q(half):
                cols = slice(2 * half * SQ, 2 * (half + 1) * SQ)
                for row, part in ((0, 0), (1, 0), (2, 1)):
                    for hh in range(2):
                        at = 32 * row + DH * hh
                        sp.dma_start(QS[at:at + DH, hh:NH:2, cols].bitcast(F32),
                                     QD[part, hh, :, :, :, cols].rearrange("c p r n -> r (c p) n")
                                     ).then_inc(qs_loaded, 16)

            def step(b):
                nxt, prv = b.shift(1), b.shift(-1)
                if b.j == 1 and b.exists:
                    held(sp, sp_passed, (st_ready, b.group(48)))
                    stack_q(1)
                if prv.exists:
                    cols = slice(prv.ring * SQ, (prv.ring + 1) * SQ)
                    held(sp, sp_passed, (mhi_done, prv.count(1, 1)))
                    sp.dma_start(QS[96:97, :, cols].bitcast(F32), MHI[:, :].bitcast(F32)).then_inc(m_loaded, 16)
                    held(sp, sp_passed, (mlo_done, prv.count(1, 1)))
                    sp.dma_start(QS[97:98, :, cols].bitcast(F32), MLO[:, :].bitcast(F32)).then_inc(m_loaded, 16)
                if nxt.exists:
                    held(sp, sp_passed, (ks_loaded, nxt.count(48, -48)), (khi_done, nxt.count(2, 2)))
                    sp.dma_start(KD[nxt.par, 0].rearrange("(c p) r n -> (p r) c n", c=DC),
                                 KHI[:, :, :].bitcast(F32)).then_inc(khi_stored, 16)
                    held(sp, sp_passed, (klo_done, nxt.count(2, 2)))
                    sp.dma_start(KD[nxt.par, 1].rearrange("(c p) r n -> (p r) c n", c=DC),
                                 KLO[:, :, :].bitcast(F32)).then_inc(klo_stored, 16)
                if b.j == 3 and nxt.exists:
                    held(sp, sp_passed, (qs_loaded, nxt.group(2 * QS_LOADS * 16)), (qhi_done, nxt.group(DC, DC)))
                    for hh in range(2):
                        sp.dma_start(QD[0, hh].rearrange("c p r n -> (p r) c n"),
                                     QHI[64 * hh:64 * hh + 64, :, :].bitcast(F32)).then_inc(qhi_stored, 16)
                    held(sp, sp_passed, (qlo_done, nxt.group(DC, DC)))
                    for hh in range(2):
                        sp.dma_start(QD[1, hh].rearrange("c p r n -> (p r) c n"),
                                     QLO[64 * hh:64 * hh + 64, :, :].bitcast(F32)).then_inc(qlo_stored, 16)
                if nxt.exists:
                    held(sp, sp_passed, (st_ready, nxt.count(12, -36)), (khi_stored, nxt.count(16, 16)))
                    for row in (0, 2):
                        sp.dma_start(KS[32 * row:32 * row + 32, nxt.ring, :, 0:SK].bitcast(F32),
                                     KD[nxt.par, 0].rearrange("g r n -> r g n")).then_inc(ks_loaded, 16)
                    held(sp, sp_passed, (klo_stored, nxt.count(16, 16)))
                    sp.dma_start(KS[32:64, nxt.ring, :, 0:SK].bitcast(F32),
                                 KD[nxt.par, 1].rearrange("g r n -> r g n")).then_inc(ks_loaded, 16)
                if b.j == 3 and nxt.exists:
                    held(sp, sp_passed, (qhi_stored, nxt.group(32, 32)), (qlo_stored, nxt.group(32, 32)),
                         (st_ready, b.group(48, 24)))
                    stack_q(0)
                if b.shift(3).exists:
                    src = ctxT[at(b.count(1, 3), 1)].rearrange("o p (c n) -> (o p) c n", c=DC)
                    held(sp, sp_passed, (v_ready, nxt.count(3, 3)))
                    sp.dma_start(CT[:, nxt.par, :, :], src).then_inc(ct_loaded[nxt.par], 16)
                if b.j == 1 and b.exists and b.shift(GB).exists:
                    src = x[at(b.group(GB, GB), GB)].rearrange("j q d -> q j d")
                    held(sp, sp_passed, (x1_done, b.group(GB)))
                    sp.dma_start(X[:, 1 - b.gpar, :, :], src).then_inc(x_loaded[1 - b.gpar], 16)
                if b.j == 3 and b.shift(-GB).exists:
                    dst = out[at(b.group(GB, -GB), GB)].rearrange("j q d -> q j d")
                    held(sp, sp_passed, (y_done, b.group(GB, GB)))
                    sp.dma_start(dst, X1[:, 1 - b.gpar, :, :]).then_inc(out_stored, 16)

            run(sp, step)
            sp.wait_ge(out_stored, 16 * NG)

        @block.gpsimd
        def _(pool):
            pool.memset(WO[:, :, :], 0.0).then_inc(pool_zeroed, 1)
            pool.memset(QS[:, :, :].bitcast(F32), 0.0).then_inc(pool_zeroed, 1)
            pool.memset(VA[:, :, :, :, DH:VW], 1.0).then_inc(pool_zeroed, 1)
            pool.memset(MHALF[:, :], -0.5).then_inc(pool_zeroed, 1)
            pool.memset(IDENT[:, :], 0.0).then_inc(ident_done, 1)
            pool.wait_ge(ident_done, 1)
            pool.affine_select(out=IDENT[:, :], in_=IDENT[:, :], compare_op=ALU.not_equal, fill=1.0,
                               base=0, pattern=[[-1, 128]], channel_multiplier=1).then_inc(ident_done, 1)
            pool.wait_ge(tanh_done, 1)
            pool.wait_ge(w_loaded, 16 * N_WEIGHTS)
            pool.tensor_scalar(BO[:, :], BO[:, :], TG[0:SQ, 0:1], None, ALU.mult).then_inc(bo_done, 1)
            pool.wait_ge(pool_zeroed, 4)
            pool.wait_ge(bo_done, 1)

            def rstd(mv, ve, res, ve_sem, res_sem, n):
                pool.tensor_scalar(ve[:, :], mv[:, :, 1], EPS, None, ALU.add).then_inc(ve_sem, 1)
                pool.wait_ge(ve_sem, n)
                pool.tensor_tensor(res[:, :], ve[:, :], MHALF[:, :], ALU.pow).then_inc(res_sem, 1)

            def step(b):
                if b.j == 2 and b.shift(GB).exists:
                    held(pool, pool_passed, (mv1_done, b.group(GB, 2 * GB)))
                    rstd(MV1[:, :], VE1, RSTD1, ve1_done, rstd1_done, b.group(1, 2))
                if b.j == 2 and b.shift(-GB).exists:
                    held(pool, pool_passed, (mv2_done, b.group(GB)))
                    rstd(MV2[:, 1 - b.gpar], VE2, RSTD2, ve2_done, rstd2_done, b.group(1))
                if b.j == 3 and b.shift(1).exists:
                    nxt = b.shift(1)
                    pool.wait_ge(xn_done, nxt.group(GB, GB))
                    pool.tensor_tensor(X[:, nxt.gpar, :, :], X[:, nxt.gpar, :, :],
                                       BO[:, :].unsqueeze(1).to_broadcast([SQ, GB, D]), ALU.add).then_inc(xb_done, 1)
                if b.j == 3 and b.shift(-GB).exists:
                    for t in range(GB):
                        held(pool, pool_passed, (wt_done, b.group(1)), (x1b_done, b.group(GB, t - GB)))
                        pool.tensor_scalar(B2W[:, :], B2[:, :], WT[:, t:t + 1], None, ALU.mult).then_inc(b2w_done, 1)
                        pool.wait_ge(b2w_done, b.group(GB, t + 1 - GB))
                        pool.tensor_tensor(X1[:, 1 - b.gpar, t, :], X1[:, 1 - b.gpar, t, :], B2W[:, :],
                                           ALU.add).then_inc(x1b_done, 1)

            run(pool, step)

        @block.scalar
        def _(act):
            act.wait_ge(w_loaded, 16 * N_WEIGHTS)
            act.activation(TG[:, :], GATE[:, :], ACT.Tanh).then_inc(tanh_done, 1)

            def step(b):
                nxt, prv = b.shift(1), b.shift(-1)
                if prv.exists:
                    act.wait_ge(mt_ready, prv.count(1, 1))
                    if past(prv.count(32)):
                        act.wait_ge(m_loaded, prv.count(32))
                    act.activation(MHI[:, :], TR[0:NH, 0:SQ], ACT.Copy).then_inc(mhi_done, 1)
                for i in range(18):
                    if i in (1, 2) and nxt.exists:
                        c = i - 1
                        act.wait_ge(k_ready, nxt.count(2, c + 1))
                        if past(nxt.count(16)):
                            act.wait_ge(khi_stored, nxt.count(16))
                        act.activation(KHI[:, c, :], P_BANK[c][:, 0:SK], ACT.Identity,
                                       bias=BK[:, c:c + 1]).then_inc(khi_done, 1)
                    if i == 2 and b.j == 3 and nxt.exists:
                        for c in range(DC):
                            act.wait_ge(xt_ready, nxt.group(DC, c + 1))
                            act.activation(XNT[:, c, :], TR[:, 0:TOK], ACT.Copy).then_inc(xt_done, 1)
                    if i == 4 and b.j == 3 and nxt.exists:
                        for c in range(DC):
                            act.wait_ge(q_ready, nxt.group(DC, c + 1))
                            if past(nxt.group(32)):
                                act.wait_ge(qhi_stored, nxt.group(32))
                            act.activation(QHI[:, c, :], P_BANK[1 - c][:, 0:TOK], ACT.Identity,
                                           bias=BQ[:, c:c + 1]).then_inc(qhi_done, 1)
                    if i == 12 and b.j == 2 and b.shift(-GB).exists:
                        for c in range(DC):
                            act.wait_ge(x2t_ready, b.group(DC, c + 1 - DC))
                            act.activation(X2NT[:, c, :], TR[:, 0:TOK], ACT.Copy).then_inc(x2t_done, 1)
                    if 4 <= i < 16 and prv.exists:
                        u = i - 4
                        pp, k = u // KC, u % KC
                        act.wait_ge(st_ready, prv.count(12, u + 1))
                        if past(prv.count(4, pp - 3)):
                            act.wait_ge(pv_done, prv.count(4, pp - 3))
                        act.activation(PT[:, k, pp * 4 * SQ:(pp + 1) * 4 * SQ], T_BANK[u % 2][0:KN, 0:4 * SQ],
                                       ACT.Exp, scale=SCALE).then_inc(exp_done, 1)
                if b.j == 2 and b.shift(-GB).exists:
                    for m in range(FC):
                        act.wait_ge(up_ready, b.group(FC, m + 1 - FC))
                        if m == 0 and past(b.group(GB, -GB)):
                            act.wait_ge(dn_ready, b.group(GB, -GB))
                        act.activation(HT[:, m, :], P_BANK[m % 2][:, 0:TOK], ACT.Gelu_apprx_tanh,
                                       bias=B1[:, m:m + 1]).then_inc(gelu_done, 1)
                if b.j == 3 and b.shift(-GB).exists:
                    act.wait_ge(diff_done, b.group(1))
                    act.activation(ER[:, :, :], DIFF[:, :, :], ACT.Exp).then_inc(er_done, 1)

            run(act, step)

        @block.vector
        def _(dve):
            dve.memset(KS[:, :, :, :].bitcast(F32), 0.0).then_inc(dve_zeroed, 1)
            dve.wait_ge(dve_zeroed, 1)
            dve.memset(KS[96:98, :, :, :].bitcast(F32), 1.0).then_inc(dve_zeroed, 1)
            dve.memset(OT[:, :], 0.0).then_inc(dve_zeroed, 1)
            dve.memset(ZR[:, :, :], 0.0).then_inc(lg_done, 1)
            dve.memset(WT[:, :], 0.0).then_inc(y_done, GB)
            dve.wait_ge(lg_done, 1)
            dve.wait_ge(y_done, GB)
            dve.wait_ge(dve_zeroed, 3)
            dve.wait_ge(w_loaded, 16 * N_WEIGHTS)
            dve.wait_ge(tanh_done, 1)

            def step(b):
                nxt, prv, pp2 = b.shift(1), b.shift(-1), b.shift(-2)
                if prv.exists:
                    dve.wait_ge(mhi_done, prv.count(1, 1))
                    if past(prv.count(32)):
                        dve.wait_ge(m_loaded, prv.count(32))
                    dve.tensor_tensor(MLO[:, :], TR[0:NH, 0:SQ], MHI[:, :].bitcast(F32),
                                      ALU.subtract).then_inc(mlo_done, 1)
                for i in range(16):
                    if b.exists:
                        dve.wait_ge(s_ready, b.count(16, i + 1))
                        if i == 0 and past(b.count(1, -1)):
                            dve.wait_ge(mt_ready, b.count(1, -1))
                        dve.tensor_reduce(NEGM[:, b.par, i:i + 1], S_BANK[i % 2][0:SQ, 0:SK], AX.X, ALU.max,
                                          negate=True).then_inc(max_done, 1)
                    if i in (1, 2) and nxt.exists:
                        c = i - 1
                        dve.wait_ge(khi_done, nxt.count(2, c + 1))
                        if past(nxt.count(16)):
                            dve.wait_ge(klo_stored, nxt.count(16))
                        dve.scalar_tensor_tensor(out=KLO[:, c, :], in0=P_BANK[c][:, 0:SK], scalar=BK[:, c:c + 1],
                                                 in1=KHI[:, c, :].bitcast(F32), op0=ALU.add,
                                                 op1=ALU.subtract).then_inc(klo_done, 1)
                    if i == 3 and pp2.exists:
                        dve.wait_ge(wo_ready, pp2.count(1, 1))
                        dve.wait_ge(xb_done, pp2.group(1, 1))
                        if pp2.j == 0 and past(pp2.group(16, -16)):
                            dve.wait_ge(out_stored, pp2.group(16, -16))
                        x1 = X1[:, pp2.gpar, pp2.j, :]
                        dve.scalar_tensor_tensor(out=x1, in0=P_BANK[0][0:SQ, 0:D], scalar=TG[0:SQ, 0:1],
                                                 in1=X[:, pp2.gpar, pp2.j, :], op0=ALU.mult,
                                                 op1=ALU.add).then_inc(x1_done, 1)
                        dve.wait_ge(x1_done, pp2.count(1, 1))
                        dve.bn_stats(BST2[:, pp2.j, :], x1).then_inc(stats2_done, 1)
                        held(dve, dve_passed, (stats2_done, pp2.count(1, 1)))
                        if pp2.j == 0:
                            held(dve, dve_passed, (x2n_done, pp2.group(GB, -GB)))
                        dve.bn_aggr(MV2[:, pp2.gpar, pp2.j, :], BST2[:, pp2.j, :]).then_inc(mv2_done, 1)
                    if i == 4 and b.j == 3 and nxt.exists:
                        for c in range(DC):
                            dve.wait_ge(qhi_done, nxt.group(DC, c + 1))
                            if past(nxt.group(32)):
                                dve.wait_ge(qlo_stored, nxt.group(32))
                            dve.scalar_tensor_tensor(out=QLO[:, c, :], in0=P_BANK[1 - c][:, 0:TOK],
                                                     scalar=BQ[:, c:c + 1], in1=QHI[:, c, :].bitcast(F32),
                                                     op0=ALU.add, op1=ALU.subtract).then_inc(qlo_done, 1)
                    if i in (5, 7, 9) and nxt.exists:
                        k = (i - 5) // 2
                        dve.wait_ge(v_ready, nxt.count(3, k + 1))
                        if k == 0 and past(nxt.count(4, -12)):
                            dve.wait_ge(pv_done, nxt.count(4, -12))
                        dve.tensor_tensor(VA[:, nxt.ring, k, :, 0:DH],
                                          P_BANK[1 - k % 2][0:KN, 0:D].rearrange("p (h d) -> p h d", h=NH),
                                          BV[:, :].rearrange("p (h d) -> p h d", h=NH), ALU.add).then_inc(v_done, 1)
                    if i == 6 and b.j == 2 and b.shift(GB).exists:
                        ng = b.shift(GB)
                        dve.wait_ge(x_loaded[ng.gpar], b.it * 16 + (b.k // GB + 1) // 2 * 16 + 16)
                        for t in range(GB):
                            dve.bn_stats(BST1[:, t, :], X[:, ng.gpar, t, :]).then_inc(stats1_done, 1)
                        for t in range(GB):
                            held(dve, dve_passed, (stats1_done, ng.group(GB, t + 1)))
                            dve.bn_aggr(MV1[:, t, :], BST1[:, t, :]).then_inc(mv1_done, 1)
                    if i == 8 and b.j == 2 and b.shift(GB).exists:
                        ng = b.shift(GB)
                        dve.wait_ge(rstd1_done, ng.group(1, 1))
                        if past(ng.group(DC)):
                            dve.wait_ge(xt_ready, ng.group(DC))
                        for t in range(GB):
                            dve.tensor_scalar(XN[:, t, :], X[:, ng.gpar, t, :], MV1[:, t, 0:1], RSTD1[:, t:t + 1],
                                              ALU.subtract, ALU.mult).then_inc(xn_done, 1)
                    if i == 10 and b.j == 2 and b.shift(-GB).exists:
                        pg = b.shift(-GB)
                        dve.wait_ge(rstd2_done, pg.group(1, 1))
                        if past(pg.group(DC)):
                            dve.wait_ge(x2t_ready, pg.group(DC))
                        for t in range(GB):
                            dve.tensor_scalar(X2N[:, t, :], X1[:, pg.gpar, t, :], MV2[:, pg.gpar, t, 0:1], RSTD2[:, t:t + 1],
                                              ALU.subtract, ALU.mult).then_inc(x2n_done, 1)
                if prv.exists:
                    n = prv.count(1, 1)
                    held(dve, dve_passed, (pv_done, prv.count(4, 4)))
                    dve.stream_shuffle(RSUM[:, :], OT[:, 0:TOK], [DH] * 32).then_inc(rsum_done, 1)
                    dve.wait_ge(rsum_done, n)
                    dve.reciprocal(RINV[:, :], RSUM[:, :]).then_inc(rinv_done, 1)
                    dve.wait_ge(rinv_done, n)
                    if past(prv.count(1)):
                        dve.wait_ge(wo_ready, prv.count(1))
                    dve.tensor_tensor(AT[:, :, :], OT[:, 0:TOK].rearrange("p (s q) -> p s q", s=4),
                                      RINV[:, :].rearrange("p (s q) -> p s q", s=4), ALU.mult).then_inc(at_done, 1)
                if b.j == 3 and b.shift(-GB).exists:
                    pg = b.shift(-GB)
                    n = pg.group(1, 1)
                    dve.wait_ge(lg_ready, n)
                    dve.tensor_copy(LG[:, :, :], TR[0:SQ, 0:GB * NE].rearrange("p (t e) -> p t e", t=GB)
                                    ).then_inc(lg_done, 1)
                    held(dve, dve_passed, (lg_done, pg.group(1, 2)))
                    for t in range(GB):
                        dve.max(SORTED[:, t, :], LG[:, t, :]).then_inc(sort_done, 1)
                    dve.wait_ge(sort_done, pg.group(GB, GB))
                    dve.tensor_tensor(DIFF[:, :, :], SORTED[:, :, :], SORTED[:, :, 0:1].to_broadcast([SQ, GB, NE]),
                                      ALU.subtract).then_inc(diff_done, 1)
                    dve.wait_ge(er_done, n)
                    dve.tensor_reduce(ZR[:, 0, :], ER[:, :, :], AX.X, ALU.add).then_inc(zr_done, 1)
                    dve.wait_ge(zr_done, pg.group(4, 1))
                    dve.reciprocal(ZR[:, 1, :], ZR[:, 0, :]).then_inc(zr_done, 1)
                    dve.wait_ge(zr_done, pg.group(4, 2))
                    dve.tensor_tensor(PR[:, :, :], ER[:, :, 0:2], ZR[:, 1, :].unsqueeze(2).to_broadcast([SQ, GB, 2]),
                                      ALU.mult).then_inc(pr_done, 1)
                    dve.wait_ge(pr_done, n)
                    dve.tensor_reduce(ZR[:, 2, :], PR[:, :, :], AX.X, ALU.add).then_inc(zr_done, 1)
                    dve.wait_ge(zr_done, pg.group(4, 3))
                    dve.reciprocal(ZR[:, 3, :], ZR[:, 2, :]).then_inc(zr_done, 1)
                    dve.wait_ge(zr_done, pg.group(4, 4))
                    dve.tensor_tensor(WN[:, :, :], PR[:, :, :], ZR[:, 3, :].unsqueeze(2).to_broadcast([SQ, GB, 2]),
                                      ALU.mult).then_inc(wn_done, 1)
                    dve.wait_ge(wn_done, n)
                    dve.tensor_reduce(WS[:, :], WN[:, :, :], AX.X, ALU.add).then_inc(ws_done, 1)
                    dve.wait_ge(ws_done, n)
                    if past(pg.group(GB)):
                        dve.wait_ge(x1b_done, pg.group(GB))
                    dve.tensor_scalar(WT[:, :], WS[:, :], TG[0:SQ, 1:2], None, ALU.mult).then_inc(wt_done, 1)
                    dve.wait_ge(wt_done, n)
                    for t in range(GB):
                        dve.wait_ge(dn_ready, pg.group(GB, t + 1))
                        dve.wait_ge(x1b_done, pg.group(GB, t + 1))
                        y = X1[:, pg.gpar, t, :]
                        dve.scalar_tensor_tensor(out=y, in0=P_BANK[t % 2][0:SQ, 0:D], scalar=WT[:, t:t + 1],
                                                 in1=y, op0=ALU.mult, op1=ALU.add).then_inc(y_done, 1)

            run(dve, step)

        @block.tensor
        def _(pe):
            pe.wait_ge(w_loaded, 16 * N_WEIGHTS)
            pe.wait_ge(pool_zeroed, 4)
            pe.wait_ge(dve_zeroed, 3)
            pe.wait_ge(ident_done, 2)

            last = {"P0": [], "P1": [], "TR": []}

            def take(bank, read_sem, value):
                for s, n in last[bank]:
                    pe.wait_ge(s, n)
                last[bank] = [(read_sem, value)]

            def enter(b):
                last["P0"] = [(v_done, b.count(3, 2)), (y_done, b.group(GB, -2 * GB + 3 + GB))]
                last["P1"] = [(v_done, b.count(3, 3)), (y_done, b.group(GB, -2 * GB + 4 + GB))]
                last["TR"] = [(xt_done, b.group(DC, DC)), (lg_done, b.group(1, 0))]

            def step(b):
                nxt, prv, pp2 = b.shift(1), b.shift(-1), b.shift(-2)
                ng, pg = b.shift(GB), b.shift(-GB)
                if prv.exists:
                    take("TR", mlo_done, prv.count(1, 1))
                    pe.wait_ge(max_done, prv.count(16, 16))
                    pe.transpose(TR[0:NH, 0:SQ], NEGM[:, prv.par, :], IDENT[0:SQ, 0:SQ]).then_inc(mt_ready, 1)

                def scores(h):
                    if h == 0:
                        pe.wait_ge(ks_loaded, b.count(48, 48))
                        pe.wait_ge(qs_loaded, b.half(QS_LOADS * 16, QS_LOADS * 16))
                    if past(b.count(16, h - 1)):
                        pe.wait_ge(max_done, b.count(16, h - 1))
                    pe.matmul(S_BANK[h % 2][0:SQ, 0:SKP], QS[0:96, h, b.ring * SQ:(b.ring + 1) * SQ],
                              KS[0:96, b.ring, h // 2, :], start=True, stop=True).then_inc(s_ready, 1)

                def scores_t(u):
                    pp, k = u // KC, u % KC
                    if u == 0:
                        pe.wait_ge(m_loaded, prv.count(32, 32))
                    if past(prv.count(12, u - 1)):
                        pe.wait_ge(exp_done, prv.count(12, u - 1))
                    for r in range(2):
                        pair = 2 * pp + r
                        mm = pe.matmul(T_BANK[u % 2][0:KN, r * 2 * SQ:(r + 1) * 2 * SQ],
                                       KS[0:98, prv.ring, pair, k * KN:(k + 1) * KN],
                                       QS[0:98, 2 * pair:2 * pair + 2, prv.ring * SQ:(prv.ring + 1) * SQ],
                                       start=True, stop=True)
                    mm.then_inc(st_ready, 1)

                def probs_v(pp):
                    if pp == 0 and past(prv.count(1)):
                        pe.wait_ge(at_done, prv.count(1))
                    pe.wait_ge(exp_done, prv.count(12, KC * (pp + 1)))
                    if pp == 0:
                        pe.wait_ge(v_done, prv.count(3, 3))
                    for k in range(KC):
                        for j in range(4):
                            h = 4 * pp + j
                            mm = pe.matmul(OT[32 * j:32 * j + VW, pp * SQ:(pp + 1) * SQ],
                                           VA[:, prv.ring, k, h, :], PT[:, k, h * SQ:(h + 1) * SQ],
                                           start=(k == 0), stop=(k == KC - 1))
                    mm.then_inc(pv_done, 1)

                for i in range(18):
                    if i < NH and b.exists:
                        scores(i)
                    if i in (1, 2) and nxt.exists:
                        c = i - 1
                        take(f"P{c}", klo_done, nxt.count(2, c + 1))
                        if c == 0:
                            pe.wait_ge(ct_loaded[nxt.par], nxt.half(16, 16))
                        for kc in range(DC):
                            mm = pe.matmul(P_BANK[c][:, 0:SK], WK[:, kc, c * 128:(c + 1) * 128],
                                           CT[:, nxt.par, kc, :], start=(kc == 0), stop=(kc == DC - 1))
                        mm.then_inc(k_ready, 1)
                    if i == 2 and b.j == 3 and nxt.exists:
                        pe.wait_ge(xn_done, nxt.group(GB, GB))
                        for c in range(DC):
                            take("TR", xt_done, nxt.group(DC, c + 1))
                            for t in range(GB):
                                mm = pe.transpose(TR[:, t * SQ:(t + 1) * SQ], XN[:, t, c * 128:(c + 1) * 128],
                                                  IDENT[0:SQ, 0:SQ])
                            mm.then_inc(xt_ready, 1)
                    if i == 3 and pp2.exists:
                        take("P0", x1_done, pp2.count(1, 1))
                        pe.wait_ge(at_done, pp2.count(1, 1))
                        for s in range(4):
                            mm = pe.matmul(P_BANK[0][0:SQ, 0:D], AT[:, s, :], WO[:, s, :],
                                           start=(s == 0), stop=(s == 3))
                        mm.then_inc(wo_ready, 1)
                    if i == 4 and b.j == 3 and nxt.exists:
                        pe.wait_ge(xt_done, nxt.group(DC, DC))
                        for c in range(DC):
                            take(f"P{1 - c}", qlo_done, nxt.group(DC, c + 1))
                            for kc in range(DC):
                                mm = pe.matmul(P_BANK[1 - c][:, 0:TOK], WQ[:, kc, c * 128:(c + 1) * 128],
                                               XNT[:, kc, :], start=(kc == 0), stop=(kc == DC - 1))
                            mm.then_inc(q_ready, 1)
                    if i in (5, 7, 9) and nxt.exists:
                        k = (i - 5) // 2
                        take(f"P{1 - k % 2}", v_done, nxt.count(3, k + 1))
                        for kc in range(DC):
                            mm = pe.matmul(P_BANK[1 - k % 2][0:KN, 0:D], CT[:, nxt.par, kc, k * KN:(k + 1) * KN],
                                           WV[:, kc, :], start=(kc == 0), stop=(kc == DC - 1))
                        mm.then_inc(v_ready, 1)
                    if i == 12 and b.j == 2 and pg.exists:
                        pe.wait_ge(x2n_done, pg.group(GB, GB))
                        for c in range(DC):
                            take("TR", x2t_done, pg.group(DC, c + 1))
                            for t in range(GB):
                                mm = pe.transpose(TR[:, t * SQ:(t + 1) * SQ], X2N[:, t, c * 128:(c + 1) * 128],
                                                  IDENT[0:SQ, 0:SQ])
                            mm.then_inc(x2t_ready, 1)
                    if 4 <= i < 16 and prv.exists:
                        scores_t(i - 4)
                    if i in (8, 11, 14, 17) and prv.exists:
                        probs_v((i - 8) // 3)
                if b.j == 2 and pg.exists:
                    pe.wait_ge(x2t_done, pg.group(DC, DC))
                    for m in range(FC):
                        take(f"P{m % 2}", gelu_done, pg.group(FC, m + 1))
                        for kc in range(DC):
                            mm = pe.matmul(P_BANK[m % 2][:, 0:TOK], W1[:, kc, m * 128:(m + 1) * 128],
                                           X2NT[:, kc, :], start=(kc == 0), stop=(kc == DC - 1))
                        mm.then_inc(up_ready, 1)
                if b.j == 3 and pg.exists:
                    take("TR", lg_done, pg.group(1, 2))
                    for t in range(GB):
                        for kc in range(DC):
                            mm = pe.matmul(TR[0:SQ, t * NE:(t + 1) * NE], X2NT[:, kc, t * SQ:(t + 1) * SQ],
                                           WR[:, kc, :], start=(kc == 0), stop=(kc == DC - 1))
                    mm.then_inc(lg_ready, 1)
                    pe.wait_ge(gelu_done, pg.group(FC, FC))
                    for t in range(GB):
                        take(f"P{t % 2}", y_done, pg.group(GB, t + 1 + GB))
                        for kc in range(FC):
                            mm = pe.matmul(P_BANK[t % 2][0:SQ, 0:D], HT[:, kc, t * SQ:(t + 1) * SQ],
                                           W2[:, kc, :], start=(kc == 0), stop=(kc == FC - 1))
                        mm.then_inc(dn_ready, 1)

            run(pe, step, enter)


def kernel(**inputs):
    import numpy as np
    import concourse.bacc as bacc
    from concourse.bass_utils import run_bass_kernel_spmd

    def columns(v):
        return np.ascontiguousarray(np.reshape(v, (-1, 128)).T)

    def heads_apart(w):
        return np.ascontiguousarray(w.reshape(-1, DC, 4, 2, DH).transpose(0, 1, 3, 2, 4).reshape(w.shape))

    given = {n: np.asarray(v) for n, v in inputs.items()}
    laid = {
        "x": given["x"],
        "ctxT": np.ascontiguousarray(
            given["ctx_1024"].reshape(NB, SK, DC, 128).transpose(0, 3, 2, 1).reshape(NB, 128, DC * SK)),
        "g_xattn": given["g_xattn"],
        "g_ffn": given["g_ffn"],
        "wq": heads_apart(given["L0_xattn_wq"]),
        "bq": columns(heads_apart(given["L0_xattn_bq"])),
        "wk": given["L0_xattn_wk"],
        "bk": columns(given["L0_xattn_bk"]),
        "wv": given["L0_xattn_wv"],
        "bv": given["L0_xattn_bv"],
        "wo": given["L0_xattn_wo"],
        "bo": given["L0_xattn_bo"],
        "wr": given["L0_ffn_router_w"],
        "w1": given["L0_ffn_w1"],
        "b1": columns(given["L0_ffn_b1"]),
        "w2": given["L0_ffn_w2"],
        "b2": given["L0_ffn_b2"],
    }
    nc = bacc.Bacc("TRN2", target_bir_lowering=False, num_devices=1, dynamic_dma_scratch_size=1024)
    aps = {n: nc.dram_tensor(f"in_{n}", v.shape, mybir.dt.from_np(v.dtype), kind="ExternalInput").ap()
           for n, v in laid.items()}
    out = nc.dram_tensor("out_y", (NB, SQ, D), F32, kind="ExternalOutput").ap()
    build(nc, out=out, **aps)
    r = run_bass_kernel_spmd(nc, [{f"in_{n}": v for n, v in laid.items()}], core_ids=[0])
    return r.results[0]["out_y"]
```

```python
from contextlib import ExitStack

import concourse.bass as bass
from concourse import mybir

F32 = mybir.dt.float32
F32R = mybir.dt.float32r
ALU = mybir.AluOpType
ACT = mybir.ActivationFunctionType
AX = mybir.AxisListType

NB, SQ, D = 32, 112, 256
SK = 375
SKP = SK + 1
NH, DH = 16, 16
NPAIR = NH // 2
FF, NE = 1024, 8
GB = 4
NG = NB // GB
TOK = GB * SQ
DC = D // 128
FC = FF // 128
KC, KN = 3, SK // 3
SCALE = float(DH) ** -0.5
EPS = 1e-5
RING = 4
VW = DH + 1


def stages(text):
    out, head = [], 0
    for word in text.split():
        name, _, i = word.partition(".")
        if name == "s":
            i, head = head, head + 1
        out.append((name, int(i or 0)))
    assert head == NH
    return out


LIGHT = """k.0 s mt s k.1 s n1 s v.0 s st.0 n2 s st.1 wo s st.2 v.1 s st.3 pv.0 s st.4 s st.5 s st.6 pv.1 s
           st.7 s st.8 s st.9 pv.2 st.10 s st.11 s v.2 pv.3 au"""
ORDER = [stages(text) for text in (
    LIGHT,
    LIGHT + " x2n",
    """mt s k.0 s x2t.0 s k.1 x2t.1 s v.0 n1 up.0 s up.1 n2 up.2 s wo up.3 s up.4 s up.5 l1 s up.6 s up.7
       st.0 st.1 v.1 st.2 xn st.3 st.4 s pv.0 s st.5 s st.6 s st.7 pv.1  st.8 s st.9 pv.2 st.10 s st.11 v.2 pv.3 au""",
    """mt s k.0 s xt.0 s k.1 xt.1 s v.0 n1 q.0 s n2 q.1 s rt wo s st.0 st.1 rw dn.0 s st.2 v.1 s st.3 pv.0 s st.4 dn.1 s
       st.5 st.6 pv.1 s st.7 dn.2 s st.8 s st.9 pv.2 s st.10 s st.11 dn.3 v.2 pv.3 au""")]
P_USERS = ("k", "v", "wo", "up", "q", "dn")
P_OF = [{stage: n % 2 for n, stage in enumerate(x for x in order if x[0] in P_USERS)} for order in ORDER]
assert all(len(p) % 2 == 0 for p in P_OF)


class At:

    def __init__(self, it, k):
        self.it, self.k = it, k
        self.j = k % GB
        self.ring = k % RING
        self.par = k % 2
        self.gpar = (k // GB) % 2
        self.exists = not isinstance(it, int) or 0 <= k < NB

    def shift(self, d):
        return At(self.it, self.k + d)

    def count(self, per, off=0):
        return self.it * (8 * per) + self.k * per + off

    def group(self, per=1, off=0):
        return self.it * (2 * per) + (self.k // GB) * per + off

    def half(self, per, off=0):
        return self.it * (4 * per) + (self.k // 2) * per + off


def past(value):
    return not isinstance(value, int) or value > 0


def held(engine, passed, *waits):
    for s, v in waits:
        if past(v):
            engine.wait_ge(s, v)
            engine.sem_inc(passed, 1)


def build(nc, x, ctxT, g_xattn, g_ffn, wq, bq, wk, bk, wv, bv, wo, bo, wr, w1, b1, w2, b2, out):
    with ExitStack() as ctx:
        def sb(name, shape, dt=F32):
            return ctx.enter_context(nc.sbuf_tensor(name, shape, dt))

        def ps(name):
            return ctx.enter_context(nc.psum_tensor(name, [128, 512], F32))

        def sem(name):
            return ctx.enter_context(nc.semaphore(name))

        WQ = sb("WQ", [128, DC, D])
        WK = sb("WK", [128, DC, D])
        WV = sb("WV", [128, DC, D])
        WO = sb("WO", [128, DC, D])
        WR = sb("WR", [128, DC, NE])
        W1 = sb("W1", [128, DC, FF])
        W2 = sb("W2", [128, FC, D])
        BQ = sb("BQ", [128, DC])
        BK = sb("BK", [128, DC])
        B1 = sb("B1", [128, FC])
        BV = sb("BV", [KN, D])
        BO = sb("BO", [SQ, D])
        B2 = sb("B2", [SQ, D])
        GATE = sb("GATE", [128, 2])
        TG = sb("TG", [128, 2])
        IDENT = sb("IDENT", [128, 128])
        MHALF = sb("MHALF", [SQ, GB])

        X = sb("X", [SQ, 2, GB, D])
        CT = sb("CT", [128, 2, DC, SK])
        BST1 = sb("BST1", [SQ, GB, 6])
        MV1 = sb("MV1", [SQ, GB, 2])
        VE1 = sb("VE1", [SQ, GB])
        RSTD1 = sb("RSTD1", [SQ, GB])
        XN = sb("XN", [SQ, GB, D])
        XNT = sb("XNT", [128, DC, TOK])

        QHI = sb("QHI", [128, DC, TOK], F32R)
        QLO = sb("QLO", [128, DC, TOK], F32R)
        QS = sb("QS", [128, NH, RING * SQ], F32R)
        KHI = sb("KHI", [128, DC, SK], F32R)
        KLO = sb("KLO", [128, DC, SK], F32R)
        KS = sb("KS", [128, RING, NPAIR, SKP], F32R)
        VA = sb("VA", [KN, RING, KC, NH, VW])
        NEGM = sb("NEGM", [SQ, 2, NH])
        MHI = sb("MHI", [NH, SQ], F32R)
        MLO = sb("MLO", [NH, SQ], F32R)
        PT = sb("PT", [KN, KC, NH * SQ])
        AU = sb("AU", [128, TOK])
        RINV = sb("RINV", [SQ, 4, 4])
        AN = sb("AN", [SQ, 4, 4, DH])
        ANT = sb("ANT", [128, DC, SQ])

        X1 = sb("X1", [SQ, 2, GB, D])
        BST2 = sb("BST2", [SQ, GB, 6])
        MV2 = sb("MV2", [SQ, 2, GB, 2])
        VE2 = sb("VE2", [SQ, GB])
        RSTD2 = sb("RSTD2", [SQ, GB])
        X2N = sb("X2N", [SQ, GB, D])
        X2NT = sb("X2NT", [128, DC, TOK])
        HT = sb("HT", [128, FC, TOK])
        LG = sb("LG", [SQ, GB, NE])
        SORTED = sb("SORTED", [SQ, GB, NE])
        DIFF = sb("DIFF", [SQ, GB, NE])
        ER = sb("ER", [SQ, GB, NE])
        ZR = sb("ZR", [SQ, 4, GB])
        PR = sb("PR", [SQ, GB, 2])
        WN = sb("WN", [SQ, GB, 2])
        WS = sb("WS", [SQ, GB])
        WT = sb("WT", [SQ, GB])
        B2W = sb("B2W", [SQ, D])

        KD = nc.dram_tensor("k_parts", (2, 2, NPAIR, 32, SK), F32, kind="Internal").ap()
        QD = nc.dram_tensor("q_parts", (2, 2, DC, 4, DH, TOK), F32, kind="Internal").ap()

        S_BANK = [ps("S0"), ps("S1")]
        T_BANK = [ps("T0"), ps("T1")]
        P_BANK = [ps("P0"), ps("P1")]
        OT = ps("OT")
        TR = ps("TR")

        sp_passed = sem("sp_passed")
        dve_passed = sem("dve_passed")
        pool_passed = sem("pool_passed")
        w_loaded = sem("w_loaded")
        x_loaded = [sem("x_loaded0"), sem("x_loaded1")]
        ct_loaded = [sem("ct_loaded0"), sem("ct_loaded1")]
        pool_zeroed = sem("pool_zeroed")
        dve_zeroed = sem("dve_zeroed")
        tanh_done = sem("tanh_done")
        bo_done = sem("bo_done")
        ident_done = sem("ident_done")
        stats1_done = sem("stats1_done")
        mv1_done = sem("mv1_done")
        ve1_done = sem("ve1_done")
        rstd1_done = sem("rstd1_done")
        xn_done = sem("xn_done")
        xb_done = sem("xb_done")
        xt_ready = sem("xt_ready")
        xt_done = sem("xt_done")
        q_ready = sem("q_ready")
        qhi_done = sem("qhi_done")
        qlo_done = sem("qlo_done")
        qs_loaded = sem("qs_loaded")
        k_ready = sem("k_ready")
        khi_done = sem("khi_done")
        klo_done = sem("klo_done")
        ks_loaded = sem("ks_loaded")
        khi_stored = sem("khi_stored")
        klo_stored = sem("klo_stored")
        qhi_stored = sem("qhi_stored")
        qlo_stored = sem("qlo_stored")
        v_ready = sem("v_ready")
        v_done = sem("v_done")
        s_ready = sem("s_ready")
        max_done = sem("max_done")
        mt_ready = sem("mt_ready")
        mhi_done = sem("mhi_done")
        mlo_done = sem("mlo_done")
        m_loaded = sem("m_loaded")
        st_ready = sem("st_ready")
        exp_done = sem("exp_done")
        pv_done = sem("pv_done")
        au_done = sem("au_done")
        ot_turned = sem("ot_turned")
        rinv_done = sem("rinv_done")
        an_done = sem("an_done")
        an_turned = sem("an_turned")
        ant_done = sem("ant_done")
        wo_ready = sem("wo_ready")
        x1_done = sem("x1_done")
        stats2_done = sem("stats2_done")
        mv2_done = sem("mv2_done")
        ve2_done = sem("ve2_done")
        rstd2_done = sem("rstd2_done")
        x2n_done = sem("x2n_done")
        x2t_ready = sem("x2t_ready")
        x2t_done = sem("x2t_done")
        up_ready = sem("up_ready")
        gelu_done = sem("gelu_done")
        lg_ready = sem("lg_ready")
        lg_done = sem("lg_done")
        sort_done = sem("sort_done")
        diff_done = sem("diff_done")
        er_done = sem("er_done")
        zr_done = sem("zr_done")
        pr_done = sem("pr_done")
        wn_done = sem("wn_done")
        ws_done = sem("ws_done")
        wt_done = sem("wt_done")
        b2w_done = sem("b2w_done")
        x1b_done = sem("x1b_done")
        dn_ready = sem("dn_ready")
        y_done = sem("y_done")
        out_stored = sem("out_stored")

        QS_LOADS = 3 * 2
        N_WEIGHTS = 3 + 3 + 3 + 2 + 1 + 3

        block = ctx.enter_context(nc.Block())

        def run(engine, step, enter=None):
            for k in range(-2, GB):
                step(At(0, k))
            with engine.Fori(0, (NG - 2) // 2) as it:
                for k in range(GB, 3 * GB):
                    if enter and k % GB == 0:
                        enter(At(it, k))
                    step(At(it, k))
            for k in range(NB - GB, NB + GB):
                if enter and k == NB - GB:
                    enter(At(0, k))
                step(At(0, k))

        @block.sync
        def _(sp):
            for dst, src in ((WK, wk), (WV, wv), (WQ, wq)):
                sp.dma_start(dst[:, :, :], src.rearrange("(c p) n -> p c n", p=128)).then_inc(w_loaded, 16)
            sp.dma_start(CT[:, 0, :, :], ctxT[0].rearrange("p (c n) -> p c n", c=DC)).then_inc(ct_loaded[0], 16)
            sp.dma_start(X[:, 0, :, :], x[0:GB].rearrange("j q d -> q j d")).then_inc(x_loaded[0], 16)
            for dst, src in ((BQ, bq), (BK, bk), (B1, b1)):
                sp.dma_start(dst[:, :], src).then_inc(w_loaded, 16)
            for dst, src, n in ((BV, bv, KN), (BO, bo, SQ), (B2, b2, SQ)):
                sp.dma_start(dst[:, :], src.partition_broadcast(n)).then_inc(w_loaded, 16)
            for i, src in enumerate((g_xattn, g_ffn)):
                sp.dma_start(GATE[:, i:i + 1], src.partition_broadcast(128)).then_inc(w_loaded, 16)
            sp.dma_start(WO[:, :, :], wo.rearrange("(c p) n -> p c n", p=128)).then_inc(w_loaded, 16)
            sp.dma_start(WR[:, :, :], wr.rearrange("(c p) n -> p c n", p=128)).then_inc(w_loaded, 16)
            sp.dma_start(W1[:, :, :], w1.rearrange("(c p) n -> p c n", p=128)).then_inc(w_loaded, 16)
            sp.dma_start(W2[:, :, :], w2.rearrange("(c p) n -> p c n", p=128)).then_inc(w_loaded, 16)
            sp.wait_ge(pool_zeroed, 3)
            sp.wait_ge(dve_zeroed, 3)

            def at(first, n):
                return slice(first, first + n) if isinstance(first, int) else bass.ds(sp.snap(first), n)

            def stack_q(half):
                cols = slice(2 * half * SQ, 2 * (half + 1) * SQ)
                for row, part in ((0, 0), (1, 0), (2, 1)):
                    for hh in range(2):
                        at = 32 * row + DH * hh
                        sp.dma_start(QS[at:at + DH, hh:NH:2, cols].bitcast(F32),
                                     QD[part, hh, :, :, :, cols].rearrange("c p r n -> r (c p) n")
                                     ).then_inc(qs_loaded, 16)

            def step(b):
                nxt, prv = b.shift(1), b.shift(-1)
                if prv.exists:
                    cols = slice(prv.ring * SQ, (prv.ring + 1) * SQ)
                    held(sp, sp_passed, (mhi_done, prv.count(1, 1)))
                    sp.dma_start(QS[96:97, :, cols].bitcast(F32), MHI[:, :].bitcast(F32)).then_inc(m_loaded, 16)
                    held(sp, sp_passed, (mlo_done, prv.count(1, 1)))
                    sp.dma_start(QS[97:98, :, cols].bitcast(F32), MLO[:, :].bitcast(F32)).then_inc(m_loaded, 16)
                if nxt.exists:
                    held(sp, sp_passed, (ks_loaded, nxt.count(48, -48)), (khi_done, nxt.count(2, 2)))
                    sp.dma_start(KD[nxt.par, 0].rearrange("(c p) r n -> (p r) c n", c=DC),
                                 KHI[:, :, :].bitcast(F32)).then_inc(khi_stored, 16)
                    held(sp, sp_passed, (klo_done, nxt.count(2, 2)))
                    sp.dma_start(KD[nxt.par, 1].rearrange("(c p) r n -> (p r) c n", c=DC),
                                 KLO[:, :, :].bitcast(F32)).then_inc(klo_stored, 16)
                if b.j == 3 and nxt.exists:
                    held(sp, sp_passed, (qs_loaded, nxt.group(2 * QS_LOADS * 16)), (qhi_done, nxt.group(DC, DC)))
                    for hh in range(2):
                        sp.dma_start(QD[0, hh].rearrange("c p r n -> (p r) c n"),
                                     QHI[64 * hh:64 * hh + 64, :, :].bitcast(F32)).then_inc(qhi_stored, 16)
                    held(sp, sp_passed, (qlo_done, nxt.group(DC, DC)))
                    for hh in range(2):
                        sp.dma_start(QD[1, hh].rearrange("c p r n -> (p r) c n"),
                                     QLO[64 * hh:64 * hh + 64, :, :].bitcast(F32)).then_inc(qlo_stored, 16)
                if nxt.exists:
                    held(sp, sp_passed, (st_ready, nxt.count(12, -36)), (khi_stored, nxt.count(16, 16)))
                    for row in (0, 2):
                        sp.dma_start(KS[32 * row:32 * row + 32, nxt.ring, :, 0:SK].bitcast(F32),
                                     KD[nxt.par, 0].rearrange("g r n -> r g n")).then_inc(ks_loaded, 16)
                    held(sp, sp_passed, (klo_stored, nxt.count(16, 16)))
                    sp.dma_start(KS[32:64, nxt.ring, :, 0:SK].bitcast(F32),
                                 KD[nxt.par, 1].rearrange("g r n -> r g n")).then_inc(ks_loaded, 16)
                if b.j == 1 and b.exists:
                    held(sp, sp_passed, (st_ready, b.group(48)))
                    stack_q(1)
                if b.j == 3 and nxt.exists:
                    held(sp, sp_passed, (qhi_stored, nxt.group(32, 32)), (qlo_stored, nxt.group(32, 32)),
                         (st_ready, b.group(48, 24)))
                    stack_q(0)
                if b.shift(3).exists:
                    src = ctxT[at(b.count(1, 3), 1)].rearrange("o p (c n) -> (o p) c n", c=DC)
                    held(sp, sp_passed, (v_ready, nxt.count(3, 3)))
                    sp.dma_start(CT[:, nxt.par, :, :], src).then_inc(ct_loaded[nxt.par], 16)
                if b.j == 1 and b.exists and b.shift(GB).exists:
                    src = x[at(b.group(GB, GB), GB)].rearrange("j q d -> q j d")
                    held(sp, sp_passed, (x1_done, b.group(GB)))
                    sp.dma_start(X[:, 1 - b.gpar, :, :], src).then_inc(x_loaded[1 - b.gpar], 16)
                if b.j == 3 and b.shift(-GB).exists:
                    dst = out[at(b.group(GB, -GB), GB)].rearrange("j q d -> q j d")
                    held(sp, sp_passed, (y_done, b.group(GB, GB)))
                    sp.dma_start(dst, X1[:, 1 - b.gpar, :, :]).then_inc(out_stored, 16)

            run(sp, step)
            sp.wait_ge(out_stored, 16 * NG)

        @block.gpsimd
        def _(pool):
            pool.memset(QS[:, :, :].bitcast(F32), 0.0).then_inc(pool_zeroed, 1)
            pool.memset(VA[:, :, :, :, DH:VW], 1.0).then_inc(pool_zeroed, 1)
            pool.memset(MHALF[:, :], -0.5).then_inc(pool_zeroed, 1)
            pool.memset(IDENT[:, :], 0.0).then_inc(ident_done, 1)
            pool.wait_ge(ident_done, 1)
            pool.affine_select(out=IDENT[:, :], in_=IDENT[:, :], compare_op=ALU.not_equal, fill=1.0,
                               base=0, pattern=[[-1, 128]], channel_multiplier=1).then_inc(ident_done, 1)
            pool.wait_ge(tanh_done, 1)
            pool.wait_ge(w_loaded, 16 * N_WEIGHTS)
            pool.tensor_scalar(BO[:, :], BO[:, :], TG[0:SQ, 0:1], None, ALU.mult).then_inc(bo_done, 1)
            pool.wait_ge(pool_zeroed, 3)
            pool.wait_ge(bo_done, 1)

            def rstd(mv, ve, res, ve_sem, res_sem, n):
                pool.tensor_scalar(ve[:, :], mv[:, :, 1], EPS, None, ALU.add).then_inc(ve_sem, 1)
                pool.wait_ge(ve_sem, n)
                pool.tensor_tensor(res[:, :], ve[:, :], MHALF[:, :], ALU.pow).then_inc(res_sem, 1)

            def step(b):
                nxt, ng, pg = b.shift(1), b.shift(GB), b.shift(-GB)
                for op, _ in ORDER[b.j]:
                    if op == "l1" and ng.exists:
                        held(pool, pool_passed, (mv1_done, ng.group(GB, GB)))
                        rstd(MV1[:, :], VE1, RSTD1, ve1_done, rstd1_done, ng.group(1, 1))
                    if op == "x2n" and pg.exists:
                        held(pool, pool_passed, (mv2_done, pg.group(GB, GB)))
                        rstd(MV2[:, pg.gpar], VE2, RSTD2, ve2_done, rstd2_done, pg.group(1, 1))
                    if op == "rw" and pg.exists:
                        for t in range(GB):
                            held(pool, pool_passed, (wt_done, pg.group(1, 1)), (x1b_done, pg.group(GB, t)))
                            pool.tensor_scalar(B2W[:, :], B2[:, :], WT[:, t:t + 1], None, ALU.mult).then_inc(b2w_done, 1)
                            pool.wait_ge(b2w_done, pg.group(GB, t + 1))
                            pool.tensor_tensor(X1[:, pg.gpar, t, :], X1[:, pg.gpar, t, :], B2W[:, :],
                                               ALU.add).then_inc(x1b_done, 1)
                if b.j == 3 and nxt.exists:
                    pool.wait_ge(xn_done, nxt.group(GB, GB))
                    pool.tensor_tensor(X[:, nxt.gpar, :, :], X[:, nxt.gpar, :, :],
                                       BO[:, :].unsqueeze(1).to_broadcast([SQ, GB, D]), ALU.add).then_inc(xb_done, 1)

            run(pool, step)

        @block.scalar
        def _(act):
            act.wait_ge(w_loaded, 16 * N_WEIGHTS)
            act.activation(TG[:, :], GATE[:, :], ACT.Tanh).then_inc(tanh_done, 1)

            def step(b):
                nxt, prv, pp2 = b.shift(1), b.shift(-1), b.shift(-2)
                pg = b.shift(-GB)
                for stage in ORDER[b.j]:
                    op, i = stage
                    bank = P_BANK[P_OF[b.j].get(stage, 0)]
                    if op == "mt" and prv.exists:
                        act.wait_ge(mt_ready, prv.count(1, 1))
                        if past(prv.count(32)):
                            act.wait_ge(m_loaded, prv.count(32))
                        act.activation(MHI[:, :], TR[0:NH, 0:SQ], ACT.Copy).then_inc(mhi_done, 1)
                    if op == "k" and nxt.exists:
                        act.wait_ge(k_ready, nxt.count(2, i + 1))
                        if past(nxt.count(16)):
                            act.wait_ge(khi_stored, nxt.count(16))
                        act.activation(KHI[:, i, :], bank[:, 0:SK], ACT.Identity,
                                       bias=BK[:, i:i + 1]).then_inc(khi_done, 1)
                    if op == "xt" and nxt.exists:
                        act.wait_ge(xt_ready, nxt.group(DC, i + 1))
                        act.activation(XNT[:, i, :], TR[:, 0:TOK], ACT.Copy).then_inc(xt_done, 1)
                    if op == "q" and nxt.exists:
                        act.wait_ge(q_ready, nxt.group(DC, i + 1))
                        if past(nxt.group(32)):
                            act.wait_ge(qhi_stored, nxt.group(32))
                        act.activation(QHI[:, i, :], bank[:, 0:TOK], ACT.Identity,
                                       bias=BQ[:, i:i + 1]).then_inc(qhi_done, 1)
                    if op == "st" and prv.exists:
                        pp, k = i // KC, i % KC
                        act.wait_ge(st_ready, prv.count(12, i + 1))
                        if past(prv.count(4, pp - 3)):
                            act.wait_ge(pv_done, prv.count(4, pp - 3))
                        act.activation(PT[:, k, pp * 4 * SQ:(pp + 1) * 4 * SQ], T_BANK[i % 2][0:KN, 0:4 * SQ],
                                       ACT.Exp, scale=SCALE).then_inc(exp_done, 1)
                    if op == "au" and prv.exists:
                        act.wait_ge(pv_done, prv.count(4, 4))
                        if past(prv.count(1)):
                            act.wait_ge(ot_turned, prv.count(1))
                        act.activation(AU[:, :], OT[:, 0:TOK], ACT.Copy).then_inc(au_done, 1)
                    if op == "n2" and pp2.exists:
                        act.wait_ge(an_turned, pp2.count(1, 1))
                        if past(pp2.count(1)):
                            act.wait_ge(wo_ready, pp2.count(1))
                        act.activation(ANT[:, :, :], TR[:, 0:DC * SQ].rearrange("p (c q) -> p c q", c=DC),
                                       ACT.Copy).then_inc(ant_done, 1)
                    if op == "x2t" and pg.exists:
                        act.wait_ge(x2t_ready, pg.group(DC, i + 1))
                        act.activation(X2NT[:, i, :], TR[:, 0:TOK], ACT.Copy).then_inc(x2t_done, 1)
                    if op == "up" and pg.exists:
                        act.wait_ge(up_ready, pg.group(FC, i + 1))
                        if i == 0 and past(pg.group(GB)):
                            act.wait_ge(dn_ready, pg.group(GB))
                        act.activation(HT[:, i, :], bank[:, 0:TOK], ACT.Gelu_apprx_tanh,
                                       bias=B1[:, i:i + 1]).then_inc(gelu_done, 1)
                    if op == "rw" and pg.exists:
                        act.wait_ge(diff_done, pg.group(1, 1))
                        act.activation(ER[:, :, :], DIFF[:, :, :], ACT.Exp).then_inc(er_done, 1)

            run(act, step)

        @block.vector
        def _(dve):
            dve.memset(KS[:, :, :, :].bitcast(F32), 0.0).then_inc(dve_zeroed, 1)
            dve.wait_ge(dve_zeroed, 1)
            dve.memset(KS[96:98, :, :, :].bitcast(F32), 1.0).then_inc(dve_zeroed, 1)
            dve.memset(OT[:, :], 0.0).then_inc(dve_zeroed, 1)
            dve.memset(ZR[:, :, :], 0.0).then_inc(lg_done, 1)
            dve.memset(WT[:, :], 0.0).then_inc(y_done, GB)
            dve.wait_ge(lg_done, 1)
            dve.wait_ge(y_done, GB)
            dve.wait_ge(dve_zeroed, 3)
            dve.wait_ge(w_loaded, 16 * N_WEIGHTS)
            dve.wait_ge(tanh_done, 1)

            def step(b):
                nxt, prv, pp2 = b.shift(1), b.shift(-1), b.shift(-2)
                ng, pg = b.shift(GB), b.shift(-GB)
                for stage in ORDER[b.j]:
                    op, i = stage
                    bank = P_BANK[P_OF[b.j].get(stage, 0)]
                    if op == "mt" and prv.exists:
                        dve.wait_ge(mhi_done, prv.count(1, 1))
                        if past(prv.count(32)):
                            dve.wait_ge(m_loaded, prv.count(32))
                        dve.tensor_tensor(MLO[:, :], TR[0:NH, 0:SQ], MHI[:, :].bitcast(F32),
                                          ALU.subtract).then_inc(mlo_done, 1)
                    if op == "s" and b.exists:
                        dve.wait_ge(s_ready, b.count(16, i + 1))
                        if i == 0 and past(b.count(1, -1)):
                            dve.wait_ge(mt_ready, b.count(1, -1))
                        dve.tensor_reduce(NEGM[:, b.par, i:i + 1], S_BANK[i % 2][0:SQ, 0:SK], AX.X, ALU.max,
                                          negate=True).then_inc(max_done, 1)
                    if op == "k" and nxt.exists:
                        dve.wait_ge(khi_done, nxt.count(2, i + 1))
                        if past(nxt.count(16)):
                            dve.wait_ge(klo_stored, nxt.count(16))
                        dve.scalar_tensor_tensor(out=KLO[:, i, :], in0=bank[:, 0:SK], scalar=BK[:, i:i + 1],
                                                 in1=KHI[:, i, :].bitcast(F32), op0=ALU.add,
                                                 op1=ALU.subtract).then_inc(klo_done, 1)
                    if op == "q" and nxt.exists:
                        dve.wait_ge(qhi_done, nxt.group(DC, i + 1))
                        if past(nxt.group(32)):
                            dve.wait_ge(qlo_stored, nxt.group(32))
                        dve.scalar_tensor_tensor(out=QLO[:, i, :], in0=bank[:, 0:TOK],
                                                 scalar=BQ[:, i:i + 1], in1=QHI[:, i, :].bitcast(F32),
                                                 op0=ALU.add, op1=ALU.subtract).then_inc(qlo_done, 1)
                    if op == "v" and nxt.exists:
                        dve.wait_ge(v_ready, nxt.count(3, i + 1))
                        if i == 0 and past(nxt.count(4, -12)):
                            dve.wait_ge(pv_done, nxt.count(4, -12))
                        dve.tensor_tensor(VA[:, nxt.ring, i, :, 0:DH],
                                          bank[0:KN, 0:D].rearrange("p (h d) -> p h d", h=NH),
                                          BV[:, :].rearrange("p (h d) -> p h d", h=NH), ALU.add).then_inc(v_done, 1)
                    if op == "n1" and pp2.exists:
                        turned = TR[0:SQ, 0:512].rearrange("p (s j e) -> p s j e", s=4, j=4)
                        dve.wait_ge(ot_turned, pp2.count(1, 1))
                        dve.reciprocal(RINV[:, :, :], turned[:, :, :, DH]).then_inc(rinv_done, 1)
                        dve.wait_ge(rinv_done, pp2.count(1, 1))
                        if past(pp2.count(1)):
                            dve.wait_ge(an_turned, pp2.count(1))
                        dve.tensor_tensor(AN[:, :, :, :], turned[:, :, :, 0:DH],
                                          RINV[:, :, :].unsqueeze(3).to_broadcast([SQ, 4, 4, DH]),
                                          ALU.mult).then_inc(an_done, 1)
                    if op == "wo" and pp2.exists:
                        dve.wait_ge(wo_ready, pp2.count(1, 1))
                        dve.wait_ge(xb_done, pp2.group(1, 1))
                        if pp2.j == 0 and past(pp2.group(16, -16)):
                            dve.wait_ge(out_stored, pp2.group(16, -16))
                        x1 = X1[:, pp2.gpar, pp2.j, :]
                        dve.scalar_tensor_tensor(out=x1, in0=bank[0:SQ, 0:D], scalar=TG[0:SQ, 0:1],
                                                 in1=X[:, pp2.gpar, pp2.j, :], op0=ALU.mult,
                                                 op1=ALU.add).then_inc(x1_done, 1)
                        dve.wait_ge(x1_done, pp2.count(1, 1))
                        dve.bn_stats(BST2[:, pp2.j, :], x1).then_inc(stats2_done, 1)
                        held(dve, dve_passed, (stats2_done, pp2.count(1, 1)))
                        if pp2.j == 0:
                            held(dve, dve_passed, (x2n_done, pp2.group(GB, -GB)))
                        dve.bn_aggr(MV2[:, pp2.gpar, pp2.j, :], BST2[:, pp2.j, :]).then_inc(mv2_done, 1)
                    if op == "l1" and ng.exists:
                        dve.wait_ge(x_loaded[ng.gpar], b.it * 16 + (b.k // GB + 1) // 2 * 16 + 16)
                        for t in range(GB):
                            dve.bn_stats(BST1[:, t, :], X[:, ng.gpar, t, :]).then_inc(stats1_done, 1)
                        for t in range(GB):
                            held(dve, dve_passed, (stats1_done, ng.group(GB, t + 1)))
                            dve.bn_aggr(MV1[:, t, :], BST1[:, t, :]).then_inc(mv1_done, 1)
                    if op == "xn" and ng.exists:
                        dve.wait_ge(rstd1_done, ng.group(1, 1))
                        if past(ng.group(DC)):
                            dve.wait_ge(xt_ready, ng.group(DC))
                        for t in range(GB):
                            dve.tensor_scalar(XN[:, t, :], X[:, ng.gpar, t, :], MV1[:, t, 0:1], RSTD1[:, t:t + 1],
                                              ALU.subtract, ALU.mult).then_inc(xn_done, 1)
                    if op == "x2n" and pg.exists:
                        dve.wait_ge(rstd2_done, pg.group(1, 1))
                        if past(pg.group(DC)):
                            dve.wait_ge(x2t_ready, pg.group(DC))
                        for t in range(GB):
                            dve.tensor_scalar(X2N[:, t, :], X1[:, pg.gpar, t, :], MV2[:, pg.gpar, t, 0:1],
                                              RSTD2[:, t:t + 1], ALU.subtract, ALU.mult).then_inc(x2n_done, 1)
                    if op == "rt" and pg.exists:
                        dve.wait_ge(lg_ready, pg.group(1, 1))
                        dve.tensor_copy(LG[:, :, :], TR[0:SQ, 0:GB * NE].rearrange("p (t e) -> p t e", t=GB)
                                        ).then_inc(lg_done, 1)
                        held(dve, dve_passed, (lg_done, pg.group(1, 2)))
                        for t in range(GB):
                            dve.max(SORTED[:, t, :], LG[:, t, :]).then_inc(sort_done, 1)
                        dve.wait_ge(sort_done, pg.group(GB, GB))
                        dve.tensor_tensor(DIFF[:, :, :], SORTED[:, :, :], SORTED[:, :, 0:1].to_broadcast([SQ, GB, NE]),
                                          ALU.subtract).then_inc(diff_done, 1)
                    if op == "rw" and pg.exists:
                        n = pg.group(1, 1)
                        dve.wait_ge(er_done, n)
                        dve.tensor_reduce(ZR[:, 0, :], ER[:, :, :], AX.X, ALU.add).then_inc(zr_done, 1)
                        dve.wait_ge(zr_done, pg.group(4, 1))
                        dve.reciprocal(ZR[:, 1, :], ZR[:, 0, :]).then_inc(zr_done, 1)
                        dve.wait_ge(zr_done, pg.group(4, 2))
                        dve.tensor_tensor(PR[:, :, :], ER[:, :, 0:2], ZR[:, 1, :].unsqueeze(2).to_broadcast([SQ, GB, 2]),
                                          ALU.mult).then_inc(pr_done, 1)
                        dve.wait_ge(pr_done, n)
                        dve.tensor_reduce(ZR[:, 2, :], PR[:, :, :], AX.X, ALU.add).then_inc(zr_done, 1)
                        dve.wait_ge(zr_done, pg.group(4, 3))
                        dve.reciprocal(ZR[:, 3, :], ZR[:, 2, :]).then_inc(zr_done, 1)
                        dve.wait_ge(zr_done, pg.group(4, 4))
                        dve.tensor_tensor(WN[:, :, :], PR[:, :, :], ZR[:, 3, :].unsqueeze(2).to_broadcast([SQ, GB, 2]),
                                          ALU.mult).then_inc(wn_done, 1)
                        dve.wait_ge(wn_done, n)
                        dve.tensor_reduce(WS[:, :], WN[:, :, :], AX.X, ALU.add).then_inc(ws_done, 1)
                        dve.wait_ge(ws_done, n)
                        if past(pg.group(GB)):
                            dve.wait_ge(x1b_done, pg.group(GB))
                        dve.tensor_scalar(WT[:, :], WS[:, :], TG[0:SQ, 1:2], None, ALU.mult).then_inc(wt_done, 1)
                        dve.wait_ge(wt_done, n)
                    if op == "dn" and pg.exists:
                        dve.wait_ge(dn_ready, pg.group(GB, i + 1))
                        dve.wait_ge(x1b_done, pg.group(GB, i + 1))
                        y = X1[:, pg.gpar, i, :]
                        dve.scalar_tensor_tensor(out=y, in0=bank[0:SQ, 0:D], scalar=WT[:, i:i + 1],
                                                 in1=y, op0=ALU.mult, op1=ALU.add).then_inc(y_done, 1)

            run(dve, step)

        @block.tensor
        def _(pe):
            pe.wait_ge(w_loaded, 16 * N_WEIGHTS)
            pe.wait_ge(pool_zeroed, 3)
            pe.wait_ge(dve_zeroed, 3)
            pe.wait_ge(ident_done, 2)

            last = {0: [], 1: [], "TR": []}

            def take(bank, read_sem, value):
                for s, n in last[bank]:
                    pe.wait_ge(s, n)
                last[bank] = [(read_sem, value)]

            def enter(b):
                last[0] = last[1] = [(v_done, b.count(3, 3)), (qlo_done, b.group(DC, DC)), (y_done, b.group(GB))]
                last["TR"] = [(xt_done, b.group(DC, DC)), (lg_done, b.group(1)), (mlo_done, b.count(1, -1)),
                              (ant_done, b.count(1, -2))]

            def step(b):
                nxt, prv, pp2 = b.shift(1), b.shift(-1), b.shift(-2)
                pg = b.shift(-GB)
                for stage in ORDER[b.j]:
                    op, i = stage
                    p = P_OF[b.j].get(stage, 0)
                    if op == "mt" and prv.exists:
                        take("TR", mlo_done, prv.count(1, 1))
                        pe.wait_ge(max_done, prv.count(16, 16))
                        pe.transpose(TR[0:NH, 0:SQ], NEGM[:, prv.par, :], IDENT[0:SQ, 0:SQ]).then_inc(mt_ready, 1)
                    if op == "s" and b.exists:
                        if i == 0:
                            pe.wait_ge(ks_loaded, b.count(48, 48))
                            pe.wait_ge(qs_loaded, b.half(QS_LOADS * 16, QS_LOADS * 16))
                        if past(b.count(16, i - 1)):
                            pe.wait_ge(max_done, b.count(16, i - 1))
                        pe.matmul(S_BANK[i % 2][0:SQ, 0:SKP], QS[0:96, i, b.ring * SQ:(b.ring + 1) * SQ],
                                  KS[0:96, b.ring, i // 2, :], start=True, stop=True).then_inc(s_ready, 1)
                    if op == "st" and prv.exists:
                        pp, k = i // KC, i % KC
                        if i == 0:
                            pe.wait_ge(m_loaded, prv.count(32, 32))
                        if past(prv.count(12, i - 1)):
                            pe.wait_ge(exp_done, prv.count(12, i - 1))
                        for r in range(2):
                            pair = 2 * pp + r
                            mm = pe.matmul(T_BANK[i % 2][0:KN, r * 2 * SQ:(r + 1) * 2 * SQ],
                                           KS[0:98, prv.ring, pair, k * KN:(k + 1) * KN],
                                           QS[0:98, 2 * pair:2 * pair + 2, prv.ring * SQ:(prv.ring + 1) * SQ],
                                           start=True, stop=True)
                        mm.then_inc(st_ready, 1)
                    if op == "pv" and prv.exists:
                        if i == 0:
                            if past(prv.count(1)):
                                pe.wait_ge(au_done, prv.count(1))
                            pe.wait_ge(v_done, prv.count(3, 3))
                        pe.wait_ge(exp_done, prv.count(12, KC * (i + 1)))
                        for k in range(KC):
                            for j in range(4):
                                h = 4 * i + j
                                mm = pe.matmul(OT[32 * j:32 * j + VW, i * SQ:(i + 1) * SQ],
                                               VA[:, prv.ring, k, h, :], PT[:, k, h * SQ:(h + 1) * SQ],
                                               start=(k == 0), stop=(k == KC - 1))
                        mm.then_inc(pv_done, 1)
                    if op == "n1" and pp2.exists:
                        take("TR", an_done, pp2.count(1, 1))
                        pe.wait_ge(au_done, pp2.count(1, 1))
                        for s in range(4):
                            mm = pe.transpose(TR[0:SQ, s * 128:(s + 1) * 128], AU[:, s * SQ:(s + 1) * SQ],
                                              IDENT[:, :])
                        mm.then_inc(ot_turned, 1)
                    if op == "n2" and pp2.exists:
                        take("TR", ant_done, pp2.count(1, 1))
                        pe.wait_ge(an_done, pp2.count(1, 1))
                        for c in range(DC):
                            mm = pe.transpose(TR[:, c * SQ:(c + 1) * SQ],
                                              AN[:, 2 * c:2 * c + 2, :, :].rearrange("p s j d -> p (s j d)"),
                                              IDENT[0:SQ, 0:SQ])
                        mm.then_inc(an_turned, 1)
                    if op == "wo" and pp2.exists:
                        take(p, x1_done, pp2.count(1, 1))
                        pe.wait_ge(ant_done, pp2.count(1, 1))
                        for c in range(DC):
                            mm = pe.matmul(P_BANK[p][0:SQ, 0:D], ANT[:, c, :], WO[:, c, :],
                                           start=(c == 0), stop=(c == DC - 1))
                        mm.then_inc(wo_ready, 1)
                    if op == "k" and nxt.exists:
                        take(p, klo_done, nxt.count(2, i + 1))
                        if i == 0:
                            pe.wait_ge(ct_loaded[nxt.par], nxt.half(16, 16))
                        for kc in range(DC):
                            mm = pe.matmul(P_BANK[p][:, 0:SK], WK[:, kc, i * 128:(i + 1) * 128],
                                           CT[:, nxt.par, kc, :], start=(kc == 0), stop=(kc == DC - 1))
                        mm.then_inc(k_ready, 1)
                    if op == "v" and nxt.exists:
                        take(p, v_done, nxt.count(3, i + 1))
                        for kc in range(DC):
                            mm = pe.matmul(P_BANK[p][0:KN, 0:D], CT[:, nxt.par, kc, i * KN:(i + 1) * KN],
                                           WV[:, kc, :], start=(kc == 0), stop=(kc == DC - 1))
                        mm.then_inc(v_ready, 1)
                    if op == "xt" and nxt.exists:
                        take("TR", xt_done, nxt.group(DC, i + 1))
                        pe.wait_ge(xn_done, nxt.group(GB, GB))
                        for t in range(GB):
                            mm = pe.transpose(TR[:, t * SQ:(t + 1) * SQ], XN[:, t, i * 128:(i + 1) * 128],
                                              IDENT[0:SQ, 0:SQ])
                        mm.then_inc(xt_ready, 1)
                    if op == "q" and nxt.exists:
                        take(p, qlo_done, nxt.group(DC, i + 1))
                        pe.wait_ge(xt_done, nxt.group(DC, DC))
                        for kc in range(DC):
                            mm = pe.matmul(P_BANK[p][:, 0:TOK], WQ[:, kc, i * 128:(i + 1) * 128],
                                           XNT[:, kc, :], start=(kc == 0), stop=(kc == DC - 1))
                        mm.then_inc(q_ready, 1)
                    if op == "x2t" and pg.exists:
                        take("TR", x2t_done, pg.group(DC, i + 1))
                        pe.wait_ge(x2n_done, pg.group(GB, GB))
                        for t in range(GB):
                            mm = pe.transpose(TR[:, t * SQ:(t + 1) * SQ], X2N[:, t, i * 128:(i + 1) * 128],
                                              IDENT[0:SQ, 0:SQ])
                        mm.then_inc(x2t_ready, 1)
                    if op == "up" and pg.exists:
                        take(p, gelu_done, pg.group(FC, i + 1))
                        pe.wait_ge(x2t_done, pg.group(DC, DC))
                        for kc in range(DC):
                            mm = pe.matmul(P_BANK[p][:, 0:TOK], W1[:, kc, i * 128:(i + 1) * 128],
                                           X2NT[:, kc, :], start=(kc == 0), stop=(kc == DC - 1))
                        mm.then_inc(up_ready, 1)
                    if op == "rt" and pg.exists:
                        take("TR", lg_done, pg.group(1, 2))
                        for t in range(GB):
                            for kc in range(DC):
                                mm = pe.matmul(TR[0:SQ, t * NE:(t + 1) * NE], X2NT[:, kc, t * SQ:(t + 1) * SQ],
                                               WR[:, kc, :], start=(kc == 0), stop=(kc == DC - 1))
                        mm.then_inc(lg_ready, 1)
                    if op == "dn" and pg.exists:
                        take(p, y_done, pg.group(GB, i + 1 + GB))
                        pe.wait_ge(gelu_done, pg.group(FC, FC))
                        for kc in range(FC):
                            mm = pe.matmul(P_BANK[p][0:SQ, 0:D], HT[:, kc, i * SQ:(i + 1) * SQ],
                                           W2[:, kc, :], start=(kc == 0), stop=(kc == FC - 1))
                        mm.then_inc(dn_ready, 1)

            run(pe, step, enter)


def kernel(**inputs):
    import numpy as np
    import concourse.bacc as bacc
    from concourse.bass_utils import run_bass_kernel_spmd

    def columns(v):
        return np.ascontiguousarray(np.reshape(v, (-1, 128)).T)

    def heads_apart(w):
        return np.ascontiguousarray(w.reshape(-1, DC, 4, 2, DH).transpose(0, 1, 3, 2, 4).reshape(w.shape))

    given = {n: np.asarray(v) for n, v in inputs.items()}
    laid = {
        "x": given["x"],
        "ctxT": np.ascontiguousarray(
            given["ctx_1024"].reshape(NB, SK, DC, 128).transpose(0, 3, 2, 1).reshape(NB, 128, DC * SK)),
        "g_xattn": given["g_xattn"],
        "g_ffn": given["g_ffn"],
        "wq": heads_apart(given["L0_xattn_wq"]),
        "bq": columns(heads_apart(given["L0_xattn_bq"])),
        "wk": given["L0_xattn_wk"],
        "bk": columns(given["L0_xattn_bk"]),
        "wv": given["L0_xattn_wv"],
        "bv": given["L0_xattn_bv"],
        "wo": given["L0_xattn_wo"],
        "bo": given["L0_xattn_bo"],
        "wr": given["L0_ffn_router_w"],
        "w1": given["L0_ffn_w1"],
        "b1": columns(given["L0_ffn_b1"]),
        "w2": given["L0_ffn_w2"],
        "b2": given["L0_ffn_b2"],
    }
    nc = bacc.Bacc("TRN2", target_bir_lowering=False, num_devices=1, dynamic_dma_scratch_size=1024)
    aps = {n: nc.dram_tensor(f"in_{n}", v.shape, mybir.dt.from_np(v.dtype), kind="ExternalInput").ap()
           for n, v in laid.items()}
    out = nc.dram_tensor("out_y", (NB, SQ, D), F32, kind="ExternalOutput").ap()
    build(nc, out=out, **aps)
    r = run_bass_kernel_spmd(nc, [{f"in_{n}": v for n, v in laid.items()}], core_ids=[0])
    return r.results[0]["out_y"]
```

```python
from contextlib import ExitStack

import concourse.bass as bass
from concourse import mybir

F32 = mybir.dt.float32
F32R = mybir.dt.float32r
ALU = mybir.AluOpType
ACT = mybir.ActivationFunctionType
AX = mybir.AxisListType

NB, SQ, D = 32, 112, 256
SK = 375
SKP = SK + 1
NH, DH = 16, 16
NPAIR = NH // 2
FF, NE = 1024, 8
GB = 2
NG = NB // GB
TOK = GB * SQ
DC = D // 128
FC = FF // 128
KC, KN = 3, SK // 3
SCALE = float(DH) ** -0.5
EPS = 1e-5
LAG = 4
RING = 4
VW = DH + 1


def stages(text):
    out, head = [], 0
    for word in text.split():
        name, _, i = word.partition(".")
        if name == "s":
            i, head = head, head + 1
        out.append((name, int(i or 0)))
    assert head == NH
    return out


ORDER = [stages(text) for text in (
    """mt s k.0 x2t.0 s k.1 s v.0 x2t.1 v.1 st.0 s st.1 n1 st.2 s st.3 up.0 pv.0 l1 up.1 lo.0 s up.2 lo.1 n2 up.3
       lo.2 s up.4 lo.3 s up.5 lo.4 s up.6 lo.5 xn up.7 lo.6 s st.4 lo.7 st.5 rt s wo st.6 st.7 pv.1 s st.8 rx s
       st.9 s st.10 pv.2 s st.11 s v.2 pv.3 au""",
    """mt s k.0 xt.0 s k.1 s v.0 xt.1 s v.1 st.0 s n1 st.1 q.0 s st.2 q.1 n2 s dh.0 rw st.3 s wo st.4 s dn.0 st.5
       s st.6 pv.0 s v.2 st.7 s pv.1 st.8 s dh.1 s st.9 s st.10 pv.2 s st.11 dn.1 pv.3 au x2n""")]

FIRST = stages("k.0 k.1 v.0 v.1 v.2 l1" + " s" * (NH - 1) + " xn s")


def banks(order):
    users = [x for x in order if x[0] in ("k", "v", "wo", "up", "q", "dh")]
    of = {stage: n % 2 for n, stage in enumerate(users)}
    return of | {("dn", i): p for (op, i), p in of.items() if op == "dh"}


class At:

    def __init__(self, it, k):
        self.it, self.k = it, k
        self.j = k % GB
        self.ring = k % RING
        self.par = k % 2
        self.gpar = (k // GB) % 2
        self.gquad = (k // GB) % 4
        self.order = FIRST if isinstance(it, int) and k == 0 else ORDER[self.j]
        self.banks = banks(self.order)
        self.exists = not isinstance(it, int) or 0 <= k < NB

    def shift(self, d):
        return At(self.it, self.k + d)

    def count(self, per, off=0):
        return self.it * (8 * per) + self.k * per + off

    def group(self, per=1, off=0):
        return self.it * (8 // GB * per) + (self.k // GB) * per + off


def past(value):
    return not isinstance(value, int) or value > 0


def held(engine, passed, *waits):
    for s, v in waits:
        if past(v):
            engine.wait_ge(s, v)
            engine.sem_inc(passed, 1)


def build(nc, x, ctxT, g_xattn, g_ffn, wq, bq, wk, bk, wv, bv, wo, bo, wr, w1, b1, w2, b2, out):
    with ExitStack() as ctx:
        def sb(name, shape, dt=F32):
            return ctx.enter_context(nc.sbuf_tensor(name, shape, dt))

        def ps(name):
            return ctx.enter_context(nc.psum_tensor(name, [128, 512], F32))

        def sem(name):
            return ctx.enter_context(nc.semaphore(name))

        WQ = [sb("WQ_HI", [128, DC, D], F32R), sb("WQ_LO", [128, DC, D], F32R)]
        WK = [sb("WK_HI", [128, DC, D], F32R), sb("WK_LO", [128, DC, D], F32R)]
        WV = [sb("WV_HI", [128, DC, D], F32R), sb("WV_LO", [128, DC, D], F32R)]
        WO = sb("WO", [128, DC, D])
        WR = sb("WR", [128, DC, NE])
        WR2 = sb("WR2", [128, DC, 2, NE], F32R)
        W1 = [sb("W1_HI", [128, DC, FF], F32R), sb("W1_LO", [128, DC, FF], F32R)]
        W2 = [sb("W2_HI", [128, FC, D], F32R), sb("W2_LO", [128, FC, D], F32R)]
        BQ = sb("BQ", [128, DC])
        BK = sb("BK", [128, DC])
        B1 = sb("B1", [128, FC])
        BV = sb("BV", [KN, D])
        BO = sb("BO", [SQ, D])
        B2 = sb("B2", [SQ, D])
        GATE = sb("GATE", [128, 2])
        TG = sb("TG", [128, 2])
        IDENT = sb("IDENT", [128, 128])
        MHALF = sb("MHALF", [SQ, GB])

        X = sb("X", [SQ, 4, GB, D])
        CTRAW = sb("CTRAW", [128, DC, SK])
        CT = [sb("CT_HI", [128, 2, DC, SKP], F32R), sb("CT_LO", [128, 2, DC, SKP], F32R)]
        BST1 = sb("BST1", [SQ, GB, 6])
        MV1 = sb("MV1", [SQ, GB, 2])
        VE1 = sb("VE1", [SQ, GB])
        RSTD1 = sb("RSTD1", [SQ, GB])
        XN = sb("XN", [SQ, GB, D])
        XT = [sb("XT_HI", [128, DC, TOK], F32R), sb("XT_LO", [128, DC, TOK], F32R)]

        QHI = sb("QHI", [128, DC, TOK], F32R)
        QLO = sb("QLO", [128, DC, TOK], F32R)
        QS = sb("QS", [128, NH, RING * SQ], F32R)
        KHI = sb("KHI", [128, DC, SK], F32R)
        KLO = sb("KLO", [128, DC, SK], F32R)
        KS = sb("KS", [128, RING, NPAIR, SKP], F32R)
        VA = sb("VA", [KN, RING, KC, NH, VW])
        NEGM = sb("NEGM", [SQ, 2, NH])
        MHI = sb("MHI", [NH, SQ], F32R)
        MLO = sb("MLO", [NH, SQ], F32R)
        PROBS = sb("PROBS", [128, KC * NH * SQ])
        AU = sb("AU", [128, 4 * SQ])
        RINV = sb("RINV", [SQ, 4, 4])
        AN = sb("AN", [SQ, 4, 4, DH])
        ANT = sb("ANT", [128, DC, SQ])

        X1 = sb("X1", [SQ, 2, GB, D])
        BST2 = sb("BST2", [SQ, GB, 6])
        MV2 = sb("MV2", [SQ, 2, GB, 2])
        VE2 = sb("VE2", [SQ, GB])
        RSTD2 = sb("RSTD2", [SQ, GB])
        HG = sb("HG", [128, 2, TOK])
        HT = [sb("HT_HI", [128, FC, TOK], F32R), sb("HT_LO", [128, FC, TOK], F32R)]
        LG = sb("LG", [SQ, GB, NE])
        SORTED = sb("SORTED", [SQ, GB, NE])
        DIFF = sb("DIFF", [SQ, GB, NE])
        ER = sb("ER", [SQ, GB, NE])
        ZR = sb("ZR", [SQ, 4, GB])
        PR = sb("PR", [SQ, GB, 2])
        WN = sb("WN", [SQ, GB, 2])
        WS = sb("WS", [SQ, GB])
        WT = sb("WT", [SQ, GB])
        B2W = sb("B2W", [SQ, D])

        KD = nc.dram_tensor("k_parts", (2, 2, NPAIR, 32, SK), F32, kind="Internal").ap()
        QD = nc.dram_tensor("q_parts", (2, 2, DC, 4, DH, TOK), F32, kind="Internal").ap()

        S_BANK = [ps("S0"), ps("S1")]
        T_BANK = [ps("T0"), ps("T1")]
        P_BANK = [ps("P0"), ps("P1")]
        OT = ps("OT")
        TR = ps("TR")

        sp_passed = sem("sp_passed")
        dve_passed = sem("dve_passed")
        pool_passed = sem("pool_passed")
        wk_loaded = sem("wk_loaded")
        wv_loaded = sem("wv_loaded")
        wq_loaded = sem("wq_loaded")
        w1_loaded = sem("w1_loaded")
        w2_loaded = sem("w2_loaded")
        wk_split = sem("wk_split")
        wv_split = sem("wv_split")
        wq_split = sem("wq_split")
        w1_split = sem("w1_split")
        wr_split = sem("wr_split")
        w2_split = sem("w2_split")
        proj_loaded = sem("proj_loaded")
        rest_loaded = sem("rest_loaded")
        x_loaded = [sem("x_loaded0"), sem("x_loaded1")]
        ct_loaded = sem("ct_loaded")
        ct_hi_done = sem("ct_hi_done")
        ct_lo_done = sem("ct_lo_done")
        pool_zeroed = sem("pool_zeroed")
        dve_zeroed = sem("dve_zeroed")
        ones_done = sem("ones_done")
        tanh_done = sem("tanh_done")
        bo_done = sem("bo_done")
        ident_done = sem("ident_done")
        stats1_done = sem("stats1_done")
        mv1_done = sem("mv1_done")
        ve1_done = sem("ve1_done")
        rstd1_done = sem("rstd1_done")
        xn_done = sem("xn_done")
        xb_done = sem("xb_done")
        xt_ready = sem("xt_ready")
        xthi_done = sem("xthi_done")
        xtlo_done = sem("xtlo_done")
        q_ready = sem("q_ready")
        qhi_done = sem("qhi_done")
        qlo_done = sem("qlo_done")
        qs_loaded = sem("qs_loaded")
        k_ready = sem("k_ready")
        khi_done = sem("khi_done")
        klo_done = sem("klo_done")
        ks_loaded = sem("ks_loaded")
        khi_stored = sem("khi_stored")
        klo_stored = sem("klo_stored")
        qhi_stored = sem("qhi_stored")
        qlo_stored = sem("qlo_stored")
        v_ready = sem("v_ready")
        v_done = sem("v_done")
        s_ready = sem("s_ready")
        max_done = sem("max_done")
        mt_ready = sem("mt_ready")
        mhi_done = sem("mhi_done")
        mlo_done = sem("mlo_done")
        m_loaded = sem("m_loaded")
        st_ready = sem("st_ready")
        exp_done = sem("exp_done")
        pv_done = sem("pv_done")
        au_done = sem("au_done")
        ot_turned = sem("ot_turned")
        rinv_done = sem("rinv_done")
        an_done = sem("an_done")
        an_turned = sem("an_turned")
        ant_done = sem("ant_done")
        wo_ready = sem("wo_ready")
        x1_done = sem("x1_done")
        stats2_done = sem("stats2_done")
        mv2_done = sem("mv2_done")
        ve2_done = sem("ve2_done")
        rstd2_done = sem("rstd2_done")
        x2n_done = sem("x2n_done")
        x2t_ready = sem("x2t_ready")
        x2thi_done = sem("x2thi_done")
        x2tlo_done = sem("x2tlo_done")
        up_ready = sem("up_ready")
        gelu_done = sem("gelu_done")
        hthi_done = sem("hthi_done")
        htlo_done = sem("htlo_done")
        lg_ready = sem("lg_ready")
        lg_done = sem("lg_done")
        sort_done = sem("sort_done")
        diff_done = sem("diff_done")
        er_done = sem("er_done")
        zr_done = sem("zr_done")
        pr_done = sem("pr_done")
        wn_done = sem("wn_done")
        ws_done = sem("ws_done")
        wt_done = sem("wt_done")
        b2w_done = sem("b2w_done")
        x1b_done = sem("x1b_done")
        dn_ready = sem("dn_ready")
        y_done = sem("y_done")
        out_stored = sem("out_stored")

        QS_LOADS = 3 * 2
        N_PROJ = 1 + 1 + 1 + 2
        N_REST = 1 + 2 + 2
        PT = PROBS[:, :].rearrange("p (k n) -> p k n", k=KC)

        def incoming(first, chunks, width):
            return PROBS[:, first:first + chunks * width].rearrange("p (c n) -> p c n", c=chunks)

        WK_IN, WV_IN, WQ_IN = (incoming(i * DC * D, DC, D) for i in range(3))
        W1_IN = incoming(3 * DC * D, DC, FF)
        W2_FIRST = 3 * DC
        W2_IN = [incoming(0, W2_FIRST, D), incoming(3 * DC * D + DC * FF, FC - W2_FIRST, D)]

        block = ctx.enter_context(nc.Block())

        def run(engine, step, enter=None):
            for k in range(-2, LAG):
                step(At(0, k))
            with engine.Fori(0, (NB - 2 * LAG) // 8) as it:
                for k in range(LAG, LAG + 8):
                    if enter and k == LAG:
                        enter(At(it, k))
                    step(At(it, k))
            for k in range(NB - LAG, NB + LAG):
                if enter and k == NB - LAG:
                    enter(At(0, k))
                step(At(0, k))

        @block.sync
        def _(sp):
            def load(dst, src, loaded):
                sp.dma_start(dst, src).then_inc(loaded, 16)

            load(CTRAW[:, :, :], ctxT[0].rearrange("p (c n) -> p c n", c=DC), ct_loaded)
            load(WK_IN, wk.rearrange("(c p) n -> p c n", p=128), wk_loaded)
            load(BK[:, :], bk, proj_loaded)
            load(WV_IN, wv.rearrange("(c p) n -> p c n", p=128), wv_loaded)
            load(X[:, 0, :, :], x[0:GB].rearrange("j q d -> q j d"), x_loaded[0])
            load(BQ[:, :], bq, proj_loaded)
            load(BV[:, :], bv.partition_broadcast(KN), proj_loaded)
            for i, src in enumerate((g_xattn, g_ffn)):
                load(GATE[:, i:i + 1], src.partition_broadcast(128), proj_loaded)
            load(WQ_IN, wq.rearrange("(c p) n -> p c n", p=128), wq_loaded)
            load(X[:, 1, :, :], x[GB:2 * GB].rearrange("j q d -> q j d"), x_loaded[1])
            load(B1[:, :], b1, rest_loaded)
            load(BO[:, :], bo.partition_broadcast(SQ), rest_loaded)
            load(B2[:, :], b2.partition_broadcast(SQ), rest_loaded)
            for dst, src in ((WO, wo), (WR, wr)):
                load(dst[:, :, :], src.rearrange("(c p) n -> p c n", p=128), rest_loaded)
            load(W1_IN, w1.rearrange("(c p) n -> p c n", p=128), w1_loaded)
            for split in (wk_split, wv_split, wq_split):
                sp.wait_ge(split, 2)
            first = W2_FIRST * 128
            load(W2_IN[0], w2[0:first].rearrange("(c p) n -> p c n", p=128), w2_loaded)
            load(W2_IN[1], w2[first:FF].rearrange("(c p) n -> p c n", p=128), w2_loaded)
            def at(first, n):
                return slice(first, first + n) if isinstance(first, int) else bass.ds(sp.snap(first), n)

            def stack_q(g):
                cols = slice(GB * g.gpar * SQ, GB * (g.gpar + 1) * SQ)
                for row, part in ((0, 0), (1, 0), (2, 1)):
                    for hh in range(2):
                        r0 = 32 * row + DH * hh
                        sp.dma_start(QS[r0:r0 + DH, hh:NH:2, cols].bitcast(F32),
                                     QD[part, hh].rearrange("c p r n -> r (c p) n")).then_inc(qs_loaded, 16)

            def step(b):
                nxt, prv, pg = b.shift(1), b.shift(-1), b.shift(-LAG)
                if prv.exists:
                    cols = slice(prv.ring * SQ, (prv.ring + 1) * SQ)
                    held(sp, sp_passed, (mhi_done, prv.count(1, 1)))
                    sp.dma_start(QS[96:97, :, cols].bitcast(F32), MHI[:, :].bitcast(F32)).then_inc(m_loaded, 16)
                    held(sp, sp_passed, (mlo_done, prv.count(1, 1)))
                    sp.dma_start(QS[97:98, :, cols].bitcast(F32), MLO[:, :].bitcast(F32)).then_inc(m_loaded, 16)
                if nxt.exists:
                    held(sp, sp_passed, (ks_loaded, nxt.count(48, -48)), (khi_done, nxt.count(2, 2)))
                    sp.dma_start(KD[nxt.par, 0].rearrange("(c p) r n -> (p r) c n", c=DC),
                                 KHI[:, :, :].bitcast(F32)).then_inc(khi_stored, 16)
                    held(sp, sp_passed, (klo_done, nxt.count(2, 2)))
                    sp.dma_start(KD[nxt.par, 1].rearrange("(c p) r n -> (p r) c n", c=DC),
                                 KLO[:, :, :].bitcast(F32)).then_inc(klo_stored, 16)
                if b.j == 1 and nxt.exists:
                    held(sp, sp_passed, (qs_loaded, nxt.group(QS_LOADS * 16)), (qhi_done, nxt.group(DC, DC)))
                    for hh in range(2):
                        sp.dma_start(QD[0, hh].rearrange("c p r n -> (p r) c n"),
                                     QHI[64 * hh:64 * hh + 64, :, :].bitcast(F32)).then_inc(qhi_stored, 16)
                    held(sp, sp_passed, (qlo_done, nxt.group(DC, DC)))
                    for hh in range(2):
                        sp.dma_start(QD[1, hh].rearrange("c p r n -> (p r) c n"),
                                     QLO[64 * hh:64 * hh + 64, :, :].bitcast(F32)).then_inc(qlo_stored, 16)
                if nxt.exists:
                    held(sp, sp_passed, (st_ready, nxt.count(12, -36)), (khi_stored, nxt.count(16, 16)))
                    for row in (0, 2):
                        sp.dma_start(KS[32 * row:32 * row + 32, nxt.ring, :, 0:SK].bitcast(F32),
                                     KD[nxt.par, 0].rearrange("g r n -> r g n")).then_inc(ks_loaded, 16)
                    held(sp, sp_passed, (klo_stored, nxt.count(16, 16)))
                    sp.dma_start(KS[32:64, nxt.ring, :, 0:SK].bitcast(F32),
                                 KD[nxt.par, 1].rearrange("g r n -> r g n")).then_inc(ks_loaded, 16)
                if b.j == 1 and nxt.exists:
                    held(sp, sp_passed, (qhi_stored, nxt.group(32, 32)), (qlo_stored, nxt.group(32, 32)),
                         (st_ready, b.group(12 * GB)))
                    if b.k == -1:
                        sp.wait_ge(pool_zeroed, 3)
                    stack_q(nxt)
                if b.shift(3).exists:
                    src = ctxT[at(b.count(1, 3), 1)].rearrange("o p (c n) -> (o p) c n", c=DC)
                    held(sp, sp_passed, (ct_lo_done, b.count(1, 3)))
                    sp.dma_start(CTRAW[:, :, :], src).then_inc(ct_loaded, 16)
                if b.j == 0 and b.exists and b.shift(2 * GB).exists:
                    src = x[at(b.group(GB, 2 * GB), GB)].rearrange("j q d -> q j d")
                    held(sp, sp_passed, (x1_done, b.group(GB, -GB)), (xn_done, b.group(GB, GB)))
                    sp.dma_start(X[:, b.shift(2 * GB).gquad, :, :], src).then_inc(x_loaded[b.gpar], 16)
                if b.j == 1 and pg.exists:
                    dst = out[at(pg.group(GB), GB)].rearrange("j q d -> q j d")
                    held(sp, sp_passed, (y_done, pg.group(GB, 2 * GB)))
                    sp.dma_start(dst, X1[:, pg.gpar, :, :]).then_inc(out_stored, 16)

            run(sp, step)
            sp.wait_ge(out_stored, 16 * NG)

        @block.gpsimd
        def _(pool):
            pool.memset(MHALF[:, :], -0.5).then_inc(pool_zeroed, 1)
            pool.memset(VA[:, :, :, :, DH:VW], 1.0).then_inc(pool_zeroed, 1)
            pool.memset(IDENT[:, :], 0.0).then_inc(ident_done, 1)
            pool.wait_ge(ident_done, 1)
            pool.affine_select(out=IDENT[:, :], in_=IDENT[:, :], compare_op=ALU.not_equal, fill=1.0,
                               base=0, pattern=[[-1, 128]], channel_multiplier=1).then_inc(ident_done, 1)
            pool.wait_ge(pool_zeroed, 2)
            pool.wait_ge(dve_zeroed, 3)

            def rstd(mv, ve, res, ve_sem, res_sem, n):
                pool.tensor_scalar(ve[:, :], mv[:, :, 1], EPS, None, ALU.add).then_inc(ve_sem, 1)
                pool.wait_ge(ve_sem, n)
                pool.tensor_tensor(res[:, :], ve[:, :], MHALF[:, :], ALU.pow).then_inc(res_sem, 1)

            def step(b):
                nxt, nn, ng, lg, pg = b.shift(1), b.shift(2), b.shift(GB), b.shift(-GB), b.shift(-LAG)
                if b.k == -1:
                    pool.wait_ge(tanh_done, 1)
                    pool.wait_ge(rest_loaded, 16 * N_REST)
                    pool.tensor_scalar(BO[:, :], BO[:, :], TG[0:SQ, 0:1], None, ALU.mult).then_inc(bo_done, 1)
                    pool.wait_ge(bo_done, 1)
                if nn.exists:
                    held(pool, pool_passed, (v_ready, b.count(3, 3)), (ct_loaded, nn.count(16, 16)))
                    pool.tensor_copy(CT[0][:, nn.par, :, 0:SK], CTRAW[:, :, :]).then_inc(ct_hi_done, 1)
                    pool.wait_ge(ct_hi_done, nn.count(1, 1))
                    pool.tensor_tensor(CT[1][:, nn.par, :, 0:SK], CTRAW[:, :, :], CT[0][:, nn.par, :, 0:SK].bitcast(F32),
                                       ALU.subtract).then_inc(ct_lo_done, 1)
                if -1 <= b.k < RING - 1:
                    pool.wait_ge(pool_zeroed, 3)
                    pool.wait_ge(ct_lo_done, nn.count(1, 1))
                    pool.memset(KS[96:98, b.k + 1, :, :].bitcast(F32), 1.0).then_inc(ones_done, 1)
                    pool.wait_ge(ones_done, b.k + 2)
                for op, _ in b.order:
                    if op == "l1" and ng.exists:
                        held(pool, pool_passed, (mv1_done, ng.group(GB, GB)))
                        rstd(MV1[:, :], VE1, RSTD1, ve1_done, rstd1_done, ng.group(1, 1))
                    if op == "x2n" and lg.exists:
                        held(pool, pool_passed, (mv2_done, lg.group(GB, GB)))
                        rstd(MV2[:, lg.gpar], VE2, RSTD2, ve2_done, rstd2_done, lg.group(1, 1))
                    if op == "rw" and pg.exists:
                        for t in range(GB):
                            held(pool, pool_passed, (wt_done, pg.group(1, 1)), (x1b_done, pg.group(GB, t)))
                            pool.tensor_scalar(B2W[:, :], B2[:, :], WT[:, t:t + 1], None, ALU.mult).then_inc(b2w_done, 1)
                            pool.wait_ge(b2w_done, pg.group(GB, t + 1))
                            pool.tensor_tensor(X1[:, pg.gpar, t, :], X1[:, pg.gpar, t, :], B2W[:, :],
                                               ALU.add).then_inc(x1b_done, 1)
                if b.k == -2:
                    pool.memset(QS[:, :, :].bitcast(F32), 0.0).then_inc(pool_zeroed, 1)
                if b.j == 1 and nxt.exists:
                    pool.wait_ge(xn_done, nxt.group(GB, GB))
                    pool.tensor_tensor(X[:, nxt.gquad, :, :], X[:, nxt.gquad, :, :],
                                       BO[:, :].unsqueeze(1).to_broadcast([SQ, GB, D]), ALU.add).then_inc(xb_done, 1)

            run(pool, step)

        @block.scalar
        def _(act):
            for raw, parts, loaded, split in ((WK_IN, WK, wk_loaded, wk_split), (WV_IN, WV, wv_loaded, wv_split),
                                              (WQ_IN, WQ, wq_loaded, wq_split)):
                act.wait_ge(loaded, 16)
                act.activation(parts[0][:, :, :], raw, ACT.Copy).then_inc(split, 1)
            act.wait_ge(proj_loaded, 16 * N_PROJ)
            act.activation(TG[:, :], GATE[:, :], ACT.Tanh).then_inc(tanh_done, 1)

            def step(b):
                nxt, prv, pp2 = b.shift(1), b.shift(-1), b.shift(-2)
                pg = b.shift(-LAG)
                if b.k == 0:
                    act.wait_ge(w1_loaded, 16)
                    act.activation(W1[0][:, :, :], W1_IN, ACT.Copy).then_inc(w1_split, 1)
                    act.wait_ge(w2_loaded, 32)
                    for raw, chunks in zip(W2_IN, (slice(0, W2_FIRST), slice(W2_FIRST, FC))):
                        act.activation(W2[0][:, chunks, :], raw, ACT.Copy).then_inc(w2_split, 1)
                if b.k == 3:
                    act.wait_ge(rest_loaded, 16 * N_REST)
                if b.k == 1:
                    for split, n in ((wk_split, 2), (wv_split, 2), (wq_split, 2), (w1_split, 2), (w2_split, 4)):
                        act.wait_ge(split, n)
                for stage in b.order:
                    op, i = stage
                    bank = P_BANK[b.banks.get(stage, 0)]
                    if op == "mt" and prv.exists:
                        act.wait_ge(mt_ready, prv.count(1, 1))
                        if past(prv.count(32)):
                            act.wait_ge(m_loaded, prv.count(32))
                        act.activation(MHI[:, :], TR[0:NH, 0:SQ], ACT.Copy).then_inc(mhi_done, 1)
                    if op == "k" and nxt.exists:
                        act.wait_ge(k_ready, nxt.count(2, i + 1))
                        if past(nxt.count(16)):
                            act.wait_ge(khi_stored, nxt.count(16))
                        act.activation(KHI[:, i, :], bank[:, 0:SK], ACT.Identity,
                                       bias=BK[:, i:i + 1]).then_inc(khi_done, 1)
                    if op == "xt" and nxt.exists:
                        act.wait_ge(xt_ready, nxt.group(DC, i + 1))
                        if i == 0 and past(nxt.group(1, -LAG // GB)):
                            act.wait_ge(lg_ready, nxt.group(1, -LAG // GB))
                        act.activation(XT[0][:, i, :], TR[:, 0:TOK], ACT.Copy).then_inc(xthi_done, 1)
                    if op == "q" and nxt.exists:
                        act.wait_ge(q_ready, nxt.group(DC, i + 1))
                        if past(nxt.group(32)):
                            act.wait_ge(qhi_stored, nxt.group(32))
                        act.activation(QHI[:, i, :], bank[:, 0:TOK], ACT.Identity,
                                       bias=BQ[:, i:i + 1]).then_inc(qhi_done, 1)
                    if op == "st" and prv.exists:
                        pp, k = i // KC, i % KC
                        act.wait_ge(st_ready, prv.count(12, i + 1))
                        if past(prv.count(4, pp - 3)):
                            act.wait_ge(pv_done, prv.count(4, pp - 3))
                        act.activation(PT[0:KN, k, pp * 4 * SQ:(pp + 1) * 4 * SQ], T_BANK[i % 2][0:KN, 0:4 * SQ],
                                       ACT.Exp, scale=SCALE).then_inc(exp_done, 1)
                    if op == "au" and prv.exists:
                        act.wait_ge(pv_done, prv.count(4, 4))
                        if past(prv.count(1)):
                            act.wait_ge(ot_turned, prv.count(1))
                        act.activation(AU[:, :], OT[:, 0:4 * SQ], ACT.Copy).then_inc(au_done, 1)
                    if op == "n2" and pp2.exists:
                        act.wait_ge(an_turned, pp2.count(1, 1))
                        if past(pp2.count(1)):
                            act.wait_ge(wo_ready, pp2.count(1))
                        act.activation(ANT[:, :, :], TR[:, 0:DC * SQ].rearrange("p (c q) -> p c q", c=DC),
                                       ACT.Copy).then_inc(ant_done, 1)
                    if op == "x2t" and pg.exists:
                        act.wait_ge(x2t_ready, pg.group(DC, i + 1))
                        act.activation(XT[0][:, i, :], TR[:, 0:TOK], ACT.Copy).then_inc(x2thi_done, 1)
                    if op == "up" and pg.exists:
                        act.wait_ge(up_ready, pg.group(FC, i + 1))
                        if i == 0 and past(pg.group(GB)):
                            act.wait_ge(dn_ready, pg.group(GB))
                        if i >= 2:
                            act.wait_ge(htlo_done, pg.group(FC, i - 1))
                        act.activation(HG[:, i % 2, :], bank[:, 0:TOK], ACT.Gelu_apprx_tanh,
                                       bias=B1[:, i:i + 1]).then_inc(gelu_done, 1)
                        act.activation(HT[0][:, i, :], bank[:, 0:TOK], ACT.Gelu_apprx_tanh,
                                       bias=B1[:, i:i + 1]).then_inc(hthi_done, 1)
                    if op == "rx" and pg.exists:
                        act.wait_ge(diff_done, pg.group(1, 1))
                        act.activation(ER[:, :, :], DIFF[:, :, :], ACT.Exp).then_inc(er_done, 1)

            run(act, step)

        @block.vector
        def _(dve):
            dve.memset(KS[:, :, :, SK:SKP].bitcast(F32), 0.0).then_inc(dve_zeroed, 1)
            for part in CT:
                dve.memset(part[:, :, :, SK:SKP].bitcast(F32), 0.0).then_inc(dve_zeroed, 1)
            dve.memset(OT[:, :], 0.0).then_inc(dve_zeroed, 1)
            dve.memset(ZR[:, :, :], 0.0).then_inc(lg_done, 1)
            dve.memset(WT[:, :], 0.0).then_inc(y_done, GB)
            def low(raw, parts, split, n, chunks):
                dve.wait_ge(split, n)
                dve.tensor_tensor(parts[1][:, chunks, :], raw, parts[0][:, chunks, :].bitcast(F32),
                                  ALU.subtract).then_inc(split, 1)

            for raw, parts, split in ((WK_IN, WK, wk_split), (WV_IN, WV, wv_split), (WQ_IN, WQ, wq_split)):
                low(raw, parts, split, 1, slice(0, DC))
            dve.wait_ge(lg_done, 1)
            dve.wait_ge(y_done, GB)
            dve.wait_ge(dve_zeroed, 4)
            dve.wait_ge(proj_loaded, 16 * N_PROJ)
            dve.wait_ge(tanh_done, 1)

            def step(b):
                nxt, prv, pp2 = b.shift(1), b.shift(-1), b.shift(-2)
                ng, lg, pg = b.shift(GB), b.shift(-GB), b.shift(-LAG)
                if b.k == 0:
                    dve.wait_ge(rest_loaded, 16 * N_REST)
                    dve.tensor_copy(WR2[:, :, 0, :], WR[:, :, :]).then_inc(wr_split, 1)
                    dve.wait_ge(wr_split, 1)
                    dve.tensor_tensor(WR2[:, :, 1, :], WR[:, :, :], WR2[:, :, 0, :].bitcast(F32),
                                      ALU.subtract).then_inc(wr_split, 1)
                    low(W1_IN, W1, w1_split, 1, slice(0, DC))
                    low(W2_IN[0], W2, w2_split, 2, slice(0, W2_FIRST))
                    low(W2_IN[1], W2, w2_split, 3, slice(W2_FIRST, FC))
                for stage in b.order:
                    op, i = stage
                    bank = P_BANK[b.banks.get(stage, 0)]
                    if op == "mt" and prv.exists:
                        dve.wait_ge(mhi_done, prv.count(1, 1))
                        if past(prv.count(32)):
                            dve.wait_ge(m_loaded, prv.count(32))
                        dve.tensor_tensor(MLO[:, :], TR[0:NH, 0:SQ], MHI[:, :].bitcast(F32),
                                          ALU.subtract).then_inc(mlo_done, 1)
                    if op == "s" and b.exists:
                        dve.wait_ge(s_ready, b.count(16, i + 1))
                        if i == 0 and past(b.count(1, -1)):
                            dve.wait_ge(mt_ready, b.count(1, -1))
                        dve.tensor_reduce(NEGM[:, b.par, i:i + 1], S_BANK[i % 2][0:SQ, 0:SK], AX.X, ALU.max,
                                          negate=True).then_inc(max_done, 1)
                    if op == "k" and nxt.exists:
                        dve.wait_ge(khi_done, nxt.count(2, i + 1))
                        if past(nxt.count(16)):
                            dve.wait_ge(klo_stored, nxt.count(16))
                        dve.scalar_tensor_tensor(out=KLO[:, i, :], in0=bank[:, 0:SK], scalar=BK[:, i:i + 1],
                                                 in1=KHI[:, i, :].bitcast(F32), op0=ALU.add,
                                                 op1=ALU.subtract).then_inc(klo_done, 1)
                    if op == "q" and nxt.exists:
                        dve.wait_ge(qhi_done, nxt.group(DC, i + 1))
                        if past(nxt.group(32)):
                            dve.wait_ge(qlo_stored, nxt.group(32))
                        dve.scalar_tensor_tensor(out=QLO[:, i, :], in0=bank[:, 0:TOK],
                                                 scalar=BQ[:, i:i + 1], in1=QHI[:, i, :].bitcast(F32),
                                                 op0=ALU.add, op1=ALU.subtract).then_inc(qlo_done, 1)
                    if op == "v" and nxt.exists:
                        dve.wait_ge(v_ready, nxt.count(3, i + 1))
                        if i == 0 and past(nxt.count(4, -12)):
                            dve.wait_ge(pv_done, nxt.count(4, -12))
                        dve.tensor_tensor(VA[:, nxt.ring, i, :, 0:DH],
                                          bank[0:KN, 0:D].rearrange("p (h d) -> p h d", h=NH),
                                          BV[:, :].rearrange("p (h d) -> p h d", h=NH), ALU.add).then_inc(v_done, 1)
                    if op == "n1" and pp2.exists:
                        turned = TR[0:SQ, 0:512].rearrange("p (s j e) -> p s j e", s=4, j=4)
                        dve.wait_ge(ot_turned, pp2.count(1, 1))
                        dve.reciprocal(RINV[:, :, :], turned[:, :, :, DH]).then_inc(rinv_done, 1)
                        dve.wait_ge(rinv_done, pp2.count(1, 1))
                        if past(pp2.count(1)):
                            dve.wait_ge(an_turned, pp2.count(1))
                        dve.tensor_tensor(AN[:, :, :, :], turned[:, :, :, 0:DH],
                                          RINV[:, :, :].unsqueeze(3).to_broadcast([SQ, 4, 4, DH]),
                                          ALU.mult).then_inc(an_done, 1)
                    if op == "wo" and pp2.exists:
                        dve.wait_ge(wo_ready, pp2.count(1, 1))
                        dve.wait_ge(xb_done, pp2.group(1, 1))
                        if pp2.j == 0 and past(pp2.group(16, -16)):
                            dve.wait_ge(out_stored, pp2.group(16, -16))
                        x1 = X1[:, pp2.gpar, pp2.j, :]
                        dve.scalar_tensor_tensor(out=x1, in0=bank[0:SQ, 0:D], scalar=TG[0:SQ, 0:1],
                                                 in1=X[:, pp2.gquad, pp2.j, :], op0=ALU.mult,
                                                 op1=ALU.add).then_inc(x1_done, 1)
                        dve.wait_ge(x1_done, pp2.count(1, 1))
                        dve.bn_stats(BST2[:, pp2.j, :], x1).then_inc(stats2_done, 1)
                        held(dve, dve_passed, (stats2_done, pp2.count(1, 1)))
                        if pp2.j == 0:
                            held(dve, dve_passed, (x2n_done, pp2.group(GB, -GB)))
                        dve.bn_aggr(MV2[:, pp2.gpar, pp2.j, :], BST2[:, pp2.j, :]).then_inc(mv2_done, 1)
                    if op == "l1" and ng.exists:
                        dve.wait_ge(x_loaded[ng.gpar], ng.it * (8 // GB // 2 * 16) + ng.k // GB // 2 * 16 + 16)
                        for t in range(GB):
                            dve.bn_stats(BST1[:, t, :], X[:, ng.gquad, t, :]).then_inc(stats1_done, 1)
                        for t in range(GB):
                            held(dve, dve_passed, (stats1_done, ng.group(GB, t + 1)))
                            dve.bn_aggr(MV1[:, t, :], BST1[:, t, :]).then_inc(mv1_done, 1)
                    if op == "xn" and ng.exists:
                        dve.wait_ge(rstd1_done, ng.group(1, 1))
                        for t in range(GB):
                            dve.tensor_scalar(XN[:, t, :], X[:, ng.gquad, t, :], MV1[:, t, 0:1], RSTD1[:, t:t + 1],
                                              ALU.subtract, ALU.mult).then_inc(xn_done, 1)
                    if op in ("xt", "x2t"):
                        g, ready, done = (nxt, xthi_done, xtlo_done) if op == "xt" else (pg, x2thi_done, x2tlo_done)
                        if g.exists:
                            dve.wait_ge(ready, g.group(DC, i + 1))
                            dve.tensor_tensor(XT[1][:, i, :], TR[:, 0:TOK], XT[0][:, i, :].bitcast(F32),
                                              ALU.subtract).then_inc(done, 1)
                    if op == "lo" and pg.exists:
                        dve.wait_ge(hthi_done, pg.group(FC, i + 1))
                        dve.tensor_tensor(HT[1][:, i, :], HG[:, i % 2, :], HT[0][:, i, :].bitcast(F32),
                                          ALU.subtract).then_inc(htlo_done, 1)
                    if op == "x2n" and lg.exists:
                        dve.wait_ge(rstd2_done, lg.group(1, 1))
                        for t in range(GB):
                            dve.tensor_scalar(XN[:, t, :], X1[:, lg.gpar, t, :], MV2[:, lg.gpar, t, 0:1],
                                              RSTD2[:, t:t + 1], ALU.subtract, ALU.mult).then_inc(x2n_done, 1)
                    if op == "rt" and pg.exists:
                        dve.wait_ge(lg_ready, pg.group(1, 1))
                        dve.tensor_reduce(LG[:, :, :],
                                          TR[0:SQ, 0:GB * 2 * NE].rearrange("p (t h e) -> p t e h", t=GB, h=2),
                                          AX.X, ALU.add).then_inc(lg_done, 1)
                        held(dve, dve_passed, (lg_done, pg.group(1, 2)))
                        for t in range(GB):
                            dve.max(SORTED[:, t, :], LG[:, t, :]).then_inc(sort_done, 1)
                        dve.wait_ge(sort_done, pg.group(GB, GB))
                        dve.tensor_tensor(DIFF[:, :, :], SORTED[:, :, :], SORTED[:, :, 0:1].to_broadcast([SQ, GB, NE]),
                                          ALU.subtract).then_inc(diff_done, 1)
                    if op == "rw" and pg.exists:
                        n = pg.group(1, 1)
                        dve.wait_ge(er_done, n)
                        dve.tensor_reduce(ZR[:, 0, :], ER[:, :, :], AX.X, ALU.add).then_inc(zr_done, 1)
                        dve.wait_ge(zr_done, pg.group(4, 1))
                        dve.reciprocal(ZR[:, 1, :], ZR[:, 0, :]).then_inc(zr_done, 1)
                        dve.wait_ge(zr_done, pg.group(4, 2))
                        dve.tensor_tensor(PR[:, :, :], ER[:, :, 0:2], ZR[:, 1, :].unsqueeze(2).to_broadcast([SQ, GB, 2]),
                                          ALU.mult).then_inc(pr_done, 1)
                        dve.wait_ge(pr_done, n)
                        dve.tensor_reduce(ZR[:, 2, :], PR[:, :, :], AX.X, ALU.add).then_inc(zr_done, 1)
                        dve.wait_ge(zr_done, pg.group(4, 3))
                        dve.reciprocal(ZR[:, 3, :], ZR[:, 2, :]).then_inc(zr_done, 1)
                        dve.wait_ge(zr_done, pg.group(4, 4))
                        dve.tensor_tensor(WN[:, :, :], PR[:, :, :], ZR[:, 3, :].unsqueeze(2).to_broadcast([SQ, GB, 2]),
                                          ALU.mult).then_inc(wn_done, 1)
                        dve.wait_ge(wn_done, n)
                        dve.tensor_reduce(WS[:, :], WN[:, :, :], AX.X, ALU.add).then_inc(ws_done, 1)
                        dve.wait_ge(ws_done, n)
                        if past(pg.group(GB)):
                            dve.wait_ge(x1b_done, pg.group(GB))
                        dve.tensor_scalar(WT[:, :], WS[:, :], TG[0:SQ, 1:2], None, ALU.mult).then_inc(wt_done, 1)
                        dve.wait_ge(wt_done, n)
                    if op == "dn" and pg.exists:
                        dve.wait_ge(dn_ready, pg.group(GB, i + 1))
                        dve.wait_ge(x1b_done, pg.group(GB, i + 1))
                        y = X1[:, pg.gpar, i, :]
                        dve.scalar_tensor_tensor(out=y, in0=bank[0:SQ, 0:D], scalar=WT[:, i:i + 1],
                                                 in1=y, op0=ALU.mult, op1=ALU.add).then_inc(y_done, 1)

            run(dve, step)

        @block.tensor
        def _(pe):
            pe.wait_ge(dve_zeroed, 4)
            pe.wait_ge(ident_done, 2)
            pe.wait_ge(wk_split, 2)
            pe.wait_ge(wv_split, 2)
            pe.wait_ge(proj_loaded, 16 * N_PROJ)

            last = {0: [], 1: [], "TR": []}

            def take(bank, read_sem, value):
                for s, n in last[bank]:
                    pe.wait_ge(s, n)
                last[bank] = [(read_sem, value)]

            def exact(out, lhs, rhs, chunks=range(DC), first=0, last=DC - 1):
                for c in chunks:
                    for n, (a, w) in enumerate(((0, 0), (0, 1), (1, 0))):
                        mm = pe.matmul(out, lhs(a, c), rhs(w, c), start=(c == first and n == 0),
                                       stop=(c == last and n == 2))
                return mm

            def enter(b):
                last[0] = last[1] = [(v_done, b.count(3, 3)), (qlo_done, b.group(DC, DC)), (y_done, b.group(GB, -GB))]
                last["TR"] = [(xtlo_done, b.group(DC, DC)), (lg_done, b.group(1, -1)), (mlo_done, b.count(1, -1)),
                              (ant_done, b.count(1, -2))]

            def step(b):
                nxt, prv, pp2 = b.shift(1), b.shift(-1), b.shift(-2)
                pg = b.shift(-LAG)
                if b.k == -1:
                    pe.wait_ge(wq_split, 2)
                if 1 <= b.k < LAG:
                    pe.wait_ge(ones_done, b.k)
                if b.k == 2:
                    pe.wait_ge(rest_loaded, 16 * N_REST)
                if b.k == 3:
                    pe.wait_ge(ones_done, RING)
                    pe.wait_ge(wr_split, 2)
                    pe.wait_ge(w1_split, 2)
                    pe.wait_ge(w2_split, 4)
                for stage in b.order:
                    op, i = stage
                    p = b.banks.get(stage, 0)
                    if op == "mt" and prv.exists:
                        take("TR", mlo_done, prv.count(1, 1))
                        pe.wait_ge(max_done, prv.count(16, 16))
                        pe.transpose(TR[0:NH, 0:SQ], NEGM[:, prv.par, :], IDENT[0:SQ, 0:SQ]).then_inc(mt_ready, 1)
                    if op == "s" and b.exists:
                        if i == 0:
                            if b.k == 0:
                                pe.wait_ge(pool_zeroed, 3)
                            pe.wait_ge(ks_loaded, b.count(48, 48))
                            pe.wait_ge(qs_loaded, b.group(QS_LOADS * 16, QS_LOADS * 16))
                        if past(b.count(16, i - 1)):
                            pe.wait_ge(max_done, b.count(16, i - 1))
                        pe.matmul(S_BANK[i % 2][0:SQ, 0:SKP], QS[0:96, i, b.ring * SQ:(b.ring + 1) * SQ],
                                  KS[0:96, b.ring, i // 2, :], start=True, stop=True).then_inc(s_ready, 1)
                    if op == "st" and prv.exists:
                        pp, k = i // KC, i % KC
                        if i == 0:
                            pe.wait_ge(m_loaded, prv.count(32, 32))
                        if past(prv.count(12, i - 1)):
                            pe.wait_ge(exp_done, prv.count(12, i - 1))
                        for r in range(2):
                            pair = 2 * pp + r
                            mm = pe.matmul(T_BANK[i % 2][0:KN, r * 2 * SQ:(r + 1) * 2 * SQ],
                                           KS[0:98, prv.ring, pair, k * KN:(k + 1) * KN],
                                           QS[0:98, 2 * pair:2 * pair + 2, prv.ring * SQ:(prv.ring + 1) * SQ],
                                           start=True, stop=True)
                        mm.then_inc(st_ready, 1)
                    if op == "pv" and prv.exists:
                        if i == 0:
                            if past(prv.count(1)):
                                pe.wait_ge(au_done, prv.count(1))
                            pe.wait_ge(v_done, prv.count(3, 3))
                        pe.wait_ge(exp_done, prv.count(12, KC * (i + 1)))
                        for k in range(KC):
                            for j in range(4):
                                h = 4 * i + j
                                mm = pe.matmul(OT[32 * j:32 * j + VW, i * SQ:(i + 1) * SQ],
                                               VA[:, prv.ring, k, h, :], PT[0:KN, k, h * SQ:(h + 1) * SQ],
                                               start=(k == 0), stop=(k == KC - 1))
                        mm.then_inc(pv_done, 1)
                    if op == "n1" and pp2.exists:
                        take("TR", an_done, pp2.count(1, 1))
                        pe.wait_ge(au_done, pp2.count(1, 1))
                        for s in range(4):
                            mm = pe.transpose(TR[0:SQ, s * 128:(s + 1) * 128], AU[:, s * SQ:(s + 1) * SQ],
                                              IDENT[:, :])
                        mm.then_inc(ot_turned, 1)
                    if op == "n2" and pp2.exists:
                        take("TR", ant_done, pp2.count(1, 1))
                        pe.wait_ge(an_done, pp2.count(1, 1))
                        for c in range(DC):
                            mm = pe.transpose(TR[:, c * SQ:(c + 1) * SQ],
                                              AN[:, 2 * c:2 * c + 2, :, :].rearrange("p s j d -> p (s j d)"),
                                              IDENT[0:SQ, 0:SQ])
                        mm.then_inc(an_turned, 1)
                    if op == "wo" and pp2.exists:
                        take(p, x1_done, pp2.count(1, 1))
                        pe.wait_ge(ant_done, pp2.count(1, 1))
                        for c in range(DC):
                            mm = pe.matmul(P_BANK[p][0:SQ, 0:D], ANT[:, c, :], WO[:, c, :],
                                           start=(c == 0), stop=(c == DC - 1))
                        mm.then_inc(wo_ready, 1)
                    if op == "k" and nxt.exists:
                        take(p, klo_done, nxt.count(2, i + 1))
                        if i == 0:
                            pe.wait_ge(ct_lo_done, nxt.count(1, 1))
                        exact(P_BANK[p][:, 0:SKP], lambda part, c: WK[part][:, c, i * 128:(i + 1) * 128],
                              lambda part, c: CT[part][:, nxt.par, c, :]).then_inc(k_ready, 1)
                    if op == "v" and nxt.exists:
                        take(p, v_done, nxt.count(3, i + 1))
                        exact(P_BANK[p][0:KN, 0:D], lambda part, c: CT[part][:, nxt.par, c, i * KN:(i + 1) * KN],
                              lambda part, c: WV[part][:, c, :]).then_inc(v_ready, 1)
                    if op == "xt" and nxt.exists:
                        take("TR", xtlo_done, nxt.group(DC, i + 1))
                        pe.wait_ge(xn_done, nxt.group(GB, GB))
                        for t in range(GB):
                            mm = pe.transpose(TR[:, t * SQ:(t + 1) * SQ], XN[:, t, i * 128:(i + 1) * 128],
                                              IDENT[0:SQ, 0:SQ])
                        mm.then_inc(xt_ready, 1)
                    if op == "q" and nxt.exists:
                        take(p, qlo_done, nxt.group(DC, i + 1))
                        pe.wait_ge(xtlo_done, nxt.group(DC, DC))
                        exact(P_BANK[p][:, 0:TOK], lambda part, c: WQ[part][:, c, i * 128:(i + 1) * 128],
                              lambda part, c: XT[part][:, c, :]).then_inc(q_ready, 1)
                    if op == "x2t" and pg.exists:
                        take("TR", x2tlo_done, pg.group(DC, i + 1))
                        pe.wait_ge(x2n_done, pg.group(GB, GB))
                        for t in range(GB):
                            mm = pe.transpose(TR[:, t * SQ:(t + 1) * SQ], XN[:, t, i * 128:(i + 1) * 128],
                                              IDENT[0:SQ, 0:SQ])
                        mm.then_inc(x2t_ready, 1)
                    if op == "up" and pg.exists:
                        take(p, hthi_done, pg.group(FC, i + 1))
                        pe.wait_ge(x2tlo_done, pg.group(DC, DC))
                        exact(P_BANK[p][:, 0:TOK], lambda part, c: W1[part][:, c, i * 128:(i + 1) * 128],
                              lambda part, c: XT[part][:, c, :]).then_inc(up_ready, 1)
                    if op == "rt" and pg.exists:
                        take("TR", lg_done, pg.group(1, 2))
                        for t in range(GB):
                            for n, (kc, part) in enumerate((kc, part) for kc in range(DC) for part in XT):
                                mm = pe.matmul(TR[0:SQ, t * 2 * NE:(t + 1) * 2 * NE],
                                               part[:, kc, t * SQ:(t + 1) * SQ],
                                               WR2[:, kc, :, :].rearrange("p h e -> p (h e)"),
                                               start=(n == 0), stop=(n == 2 * DC - 1))
                        mm.then_inc(lg_ready, 1)
                    if op in ("dh", "dn") and pg.exists:
                        if op == "dh":
                            take(p, y_done, pg.group(GB, i + 1 + GB))
                            pe.wait_ge(htlo_done, pg.group(FC, FC))
                        mm = exact(P_BANK[p][0:SQ, 0:D], lambda part, c: HT[part][:, c, i * SQ:(i + 1) * SQ],
                                   lambda part, c: W2[part][:, c, :],
                                   range(0, FC // 2) if op == "dh" else range(FC // 2, FC), last=FC - 1)
                        if op == "dn":
                            mm.then_inc(dn_ready, 1)

            run(pe, step, enter)


def kernel(**inputs):
    import numpy as np
    import concourse.bacc as bacc
    from concourse.bass_utils import run_bass_kernel_spmd

    def columns(v):
        return np.ascontiguousarray(np.reshape(v, (-1, 128)).T)

    def heads_apart(w):
        return np.ascontiguousarray(w.reshape(-1, DC, 4, 2, DH).transpose(0, 1, 3, 2, 4).reshape(w.shape))

    given = {n: np.asarray(v) for n, v in inputs.items()}
    laid = {
        "x": given["x"],
        "ctxT": np.ascontiguousarray(
            given["ctx_1024"].reshape(NB, SK, DC, 128).transpose(0, 3, 2, 1).reshape(NB, 128, DC * SK)),
        "g_xattn": given["g_xattn"],
        "g_ffn": given["g_ffn"],
        "wq": heads_apart(given["L0_xattn_wq"]),
        "bq": columns(heads_apart(given["L0_xattn_bq"])),
        "wk": given["L0_xattn_wk"],
        "bk": columns(given["L0_xattn_bk"]),
        "wv": given["L0_xattn_wv"],
        "bv": given["L0_xattn_bv"],
        "wo": given["L0_xattn_wo"],
        "bo": given["L0_xattn_bo"],
        "wr": given["L0_ffn_router_w"],
        "w1": given["L0_ffn_w1"],
        "b1": columns(given["L0_ffn_b1"]),
        "w2": given["L0_ffn_w2"],
        "b2": given["L0_ffn_b2"],
    }
    nc = bacc.Bacc("TRN2", target_bir_lowering=False, num_devices=1, dynamic_dma_scratch_size=1024)
    aps = {n: nc.dram_tensor(f"in_{n}", v.shape, mybir.dt.from_np(v.dtype), kind="ExternalInput").ap()
           for n, v in laid.items()}
    out = nc.dram_tensor("out_y", (NB, SQ, D), F32, kind="ExternalOutput").ap()
    build(nc, out=out, **aps)
    r = run_bass_kernel_spmd(nc, [{f"in_{n}": v for n, v in laid.items()}], core_ids=[0])
    return r.results[0]["out_y"]
```
